# Optimizing a Trainium2 kernel written in Bass

```python
import numpy as np
import jax
import jax.numpy as jnp

def _softmax(x, axis=-1):
    return jax.nn.softmax(x, axis=axis)

def _gelu(x):
    return jax.nn.gelu(x, approximate=True)

def _silu(x):
    return jax.nn.silu(x)

def _sigmoid(x):
    return jax.nn.sigmoid(x)

def _layernorm(x, axis=-1, eps=1e-05):
    m = jnp.mean(x, axis=axis, keepdims=True)
    v = jnp.var(x, axis=axis, keepdims=True)
    return (x - m) / jnp.sqrt(v + eps)

def _scatter_add(tgt, idx, src, axis=0):
    return tgt.at[idx].add(src)

def _segment_sum(src, seg, n):
    return jax.ops.segment_sum(src, seg, n)
kernel_name = 'mk_xattn_ffn_d1_seqx_r8_371e19'

def setup_inputs(seed: int=0):
    np.random.seed(seed)
    _w = jnp.asarray

    def _rec_inputs():
        import jax
        import jax.numpy as jnp
        _rk = jax.random.key(seed)
        x = 7.22e-05 + 1 * jax.random.normal(jax.random.fold_in(_rk, 1), (32, 64, 128), jnp.float32)
        _lenS = 64 - jax.random.randint(jax.random.fold_in(_rk, 7), (32,), 0, max(1, 64 // 4) + 1, jnp.int32)
        _lenS2 = 64 - jax.random.randint(jax.random.fold_in(_rk, 8), (32,), 0, max(1, 64 // 4) + 1, jnp.int32)
        _ctx_1024P = jax.random.normal(jax.random.fold_in(_rk, 11), (32, 16, 128), jnp.float32)
        _ctx_1024c = jax.random.dirichlet(jax.random.fold_in(_rk, 511), 0.3 * jnp.ones((16,), jnp.float32), (32, 64))
        _ctx_1024t = jnp.einsum('bsk,bkd->bsd', _ctx_1024c, _ctx_1024P)
        _ctx_1024t = _ctx_1024t * jax.lax.rsqrt(jnp.mean(jnp.square(_ctx_1024t)) + 1e-12) * 0.953939
        ctx_1024 = 4.13588e-05 + 0.999923 * (_ctx_1024t + 0.3 * jax.random.normal(jax.random.fold_in(_rk, 611), (32, 64, 128), jnp.float32))
        return (x, ctx_1024)
    x, ctx_1024 = _rec_inputs()

    def _L0_xattn_setup():
        import jax, jax.numpy as jnp
        import numpy as np
        R = 3.9
        STRENGTH = 0.1
        N_ITER = 10
        I0 = 1.0
        OMEGA = 1.0
        KWAVE = 2.0
        ALPHA_BASE = 1.0
        LC = 0.5
        DE = 2.0
        CHIRP_N = 1
        AMIN = 0.1
        AMAX = 3.0
        FD = 1.5
        T = 0.0
        ATT_ALPHA = 1.5
        EPS = 1e-10
        FCI = 0.7
        STAB = 0.8
        DEMAND = 0.6
        BASE = 0.5
        SENS = 1.0
        DECAY = 0.1
        B, S, D4 = (4, 256, 128)

        def hamilton(a, b):
            aw, ax, ay, az = jnp.split(a, 4, axis=-1)
            bw, bx, by, bz = jnp.split(b, 4, axis=-1)
            w = aw * bw - ax * bx - ay * by - az * bz
            x = aw * bx + ax * bw + ay * bz - az * by
            y = aw * by - ax * bz + ay * bw + az * bx
            z = aw * bz + ax * by - ay * bx + az * bw
            return jnp.concatenate([w, x, y, z], axis=-1)
        key = jax.random.key(seed)
        ks = jax.random.split(key, 8)
        sc = 0.02
        return {'query': jax.random.normal(ks[0], (B, S, D4), jnp.float32), 'memory': jax.random.normal(ks[1], (B, S, D4), jnp.float32), 'Wq': jax.random.normal(ks[2], (D4, D4), jnp.float32) * sc, 'bq': jnp.zeros((D4,), jnp.float32), 'Wk': jax.random.normal(ks[3], (D4, D4), jnp.float32) * sc, 'bk': jnp.zeros((D4,), jnp.float32), 'Wv': jax.random.normal(ks[4], (D4, D4), jnp.float32) * sc, 'bv': jnp.zeros((D4,), jnp.float32)}
    _L0_xattn_all = _L0_xattn_setup()
    _L0_xattn_in = {k: v for k, v in _L0_xattn_all.items() if k in ('Wq', 'bq', 'Wk', 'bk', 'Wv', 'bv')}
    del _L0_xattn_all

    def _L0_ffn_setup():
        import jax, jax.numpy as jnp
        import numpy as np
        D_MODEL = 128
        NUM_EXPERTS = 8
        TOP_K = 2
        B, S = (1, 256)
        key = jax.random.key(seed)
        ks = jax.random.split(key, 8)
        sd = 1.0 / np.sqrt(D_MODEL)
        x = jax.random.normal(ks[0], (B, S, D_MODEL), dtype=jnp.float32)
        gate_w = jax.random.normal(ks[1], (D_MODEL, NUM_EXPERTS), dtype=jnp.float32) * sd
        gate_b = jnp.zeros((NUM_EXPERTS,), dtype=jnp.float32)
        w1 = jax.random.normal(ks[2], (NUM_EXPERTS, D_MODEL, 8 * D_MODEL), dtype=jnp.float32) * sd
        b1 = jnp.zeros((NUM_EXPERTS, 8 * D_MODEL), dtype=jnp.float32)
        w2 = jax.random.normal(ks[3], (NUM_EXPERTS, 4 * D_MODEL, D_MODEL), dtype=jnp.float32) * (1.0 / np.sqrt(4 * D_MODEL))
        b2 = jnp.zeros((NUM_EXPERTS, D_MODEL), dtype=jnp.float32)
        return {'x': x, 'gate_w': gate_w, 'gate_b': gate_b, 'w1': w1, 'b1': b1, 'w2': w2, 'b2': b2}
    _L0_ffn_all = _L0_ffn_setup()
    _L0_ffn_in = {k: v for k, v in _L0_ffn_all.items() if k in ('gate_w', 'gate_b', 'w1', 'b1', 'w2', 'b2')}
    del _L0_ffn_all
    return {'x': x, 'ctx_1024': ctx_1024, 'L0_xattn_Wq': _L0_xattn_in['Wq'], 'L0_xattn_bq': _L0_xattn_in['bq'], 'L0_xattn_Wk': _L0_xattn_in['Wk'], 'L0_xattn_bk': _L0_xattn_in['bk'], 'L0_xattn_Wv': _L0_xattn_in['Wv'], 'L0_xattn_bv': _L0_xattn_in['bv'], 'L0_ffn_gate_w': _L0_ffn_in['gate_w'], 'L0_ffn_gate_b': _L0_ffn_in['gate_b'], 'L0_ffn_w1': _L0_ffn_in['w1'], 'L0_ffn_b1': _L0_ffn_in['b1'], 'L0_ffn_w2': _L0_ffn_in['w2'], 'L0_ffn_b2': _L0_ffn_in['b2']}

def reference(x, ctx_1024, L0_xattn_Wq, L0_xattn_bq, L0_xattn_Wk, L0_xattn_bk, L0_xattn_Wv, L0_xattn_bv, L0_ffn_gate_w, L0_ffn_gate_b, L0_ffn_w1, L0_ffn_b1, L0_ffn_w2, L0_ffn_b2):
    import jax
    import jax.numpy as jnp

    def _L0_xattn_ref(query, memory, Wq, bq, Wk, bk, Wv, bv):
        import jax, jax.numpy as jnp
        import numpy as np
        R = 3.9
        STRENGTH = 0.1
        N_ITER = 10
        I0 = 1.0
        OMEGA = 1.0
        KWAVE = 2.0
        ALPHA_BASE = 1.0
        LC = 0.5
        DE = 2.0
        CHIRP_N = 1
        AMIN = 0.1
        AMAX = 3.0
        FD = 1.5
        T = 0.0
        ATT_ALPHA = 1.5
        EPS = 1e-10
        FCI = 0.7
        STAB = 0.8
        DEMAND = 0.6
        BASE = 0.5
        SENS = 1.0
        DECAY = 0.1
        B, S, D4 = (4, 256, 128)

        def hamilton(a, b):
            aw, ax, ay, az = jnp.split(a, 4, axis=-1)
            bw, bx, by, bz = jnp.split(b, 4, axis=-1)
            w = aw * bw - ax * bx - ay * by - az * bz
            x = aw * bx + ax * bw + ay * bz - az * by
            y = aw * by - ax * bz + ay * bw + az * bx
            z = aw * bz + ax * by - ay * bx + az * bw
            return jnp.concatenate([w, x, y, z], axis=-1)
        s = jax.nn.sigmoid(jnp.linalg.norm(query, axis=-1))
        for _ in range(N_ITER):
            s = R * s * (1.0 - s)
        q = query * (1.0 + STRENGTH * (s[..., None] - 0.5))
        seq = q.shape[1]
        alpha = float(np.clip(ALPHA_BASE * (1.0 + LC * (FD - DE) / DE), AMIN, AMAX))
        beta = 2 * CHIRP_N + 1 - 2 * FD
        lam = jnp.arange(seq, dtype=q.dtype) / seq
        wave = I0 * jnp.sin(OMEGA * T + alpha * lam) * jnp.cos(OMEGA * T - KWAVE * lam + beta * lam ** 2)
        q = q * (1.0 + 0.1 * wave[None, :, None])
        dop = (1 - DECAY) * BASE + DECAY * jax.nn.sigmoid(jnp.float32(FCI * SENS))
        ser = (1 - DECAY) * BASE + DECAY * jax.nn.sigmoid(jnp.float32(STAB * SENS))
        nor = (1 - DECAY) * BASE + DECAY * jax.nn.sigmoid(jnp.float32(DEMAND * SENS))
        mem = memory * (0.4 * dop + 0.3 * ser + 0.3 * nor)
        Q = q @ Wq.T + bq
        K = mem @ Wk.T + bk
        V = mem @ Wv.T + bv
        Qf = jnp.fft.fft(Q, axis=-2)
        Kf = jnp.fft.fft(K, axis=-2)
        Vf = jnp.fft.fft(V, axis=-2)
        kidx = jnp.arange(seq, dtype=jnp.float32)
        filt = jnp.exp(1j * ATT_ALPHA * jnp.arctan(jnp.log(kidx + EPS)))[None, :, None]
        QK = hamilton(Qf * filt, Kf * filt)
        QKV = hamilton(QK, Vf * filt)
        attended = jnp.fft.ifft(QKV, axis=-2).real.astype(query.dtype)
        return attended

    def _L0_ffn_ref(x, gate_w, gate_b, w1, b1, w2, b2):
        import jax, jax.numpy as jnp
        import numpy as np
        D_MODEL = 128
        NUM_EXPERTS = 8
        TOP_K = 2
        B, S = (1, 256)
        gate_logits = jnp.einsum('bsd,de->bse', x, gate_w) + gate_b
        weights, indices = jax.lax.top_k(gate_logits, TOP_K)
        weights = jax.nn.softmax(weights, axis=-1)
        h = jnp.einsum('bsd,edh->ebsh', x, w1) + b1[:, None, None, :]
        xh, gh = jnp.split(h, 2, axis=-1)
        act = jax.nn.silu(gh) * xh
        out_e = jnp.einsum('ebsf,efd->ebsd', act, w2) + b2[:, None, None, :]
        out_e = jnp.transpose(out_e, (1, 2, 0, 3))
        sel = jnp.take_along_axis(out_e, indices[..., None], axis=2)
        return jnp.sum(sel * weights[..., None], axis=2)
    x = x + _L0_xattn_ref(_layernorm(x, axis=-1), ctx_1024, L0_xattn_Wq, L0_xattn_bq, L0_xattn_Wk, L0_xattn_bk, L0_xattn_Wv, L0_xattn_bv)
    x = x + _L0_ffn_ref(_layernorm(x, axis=-1), L0_ffn_gate_w, L0_ffn_gate_b, L0_ffn_w1, L0_ffn_b1, L0_ffn_w2, L0_ffn_b2)
    return x

_drawn_inputs = setup_inputs


def setup_inputs(seed=0):
    import zlib

    import numpy as np

    out = dict(_drawn_inputs(seed))
    spreads = {'L0_xattn_bq': (0.0, 0.1),
     'L0_xattn_bk': (0.0, 0.1),
     'L0_xattn_bv': (0.0, 0.1),
     'L0_ffn_gate_b': (0.0, 0.8),
     'L0_ffn_b1': (0.0, 0.8),
     'L0_ffn_b2': (0.0, 2.0)}
    factors = {'L0_ffn_gate_w': 3.343, 'L0_ffn_w1': 2.751, 'L0_ffn_w2': 2.906}
    for name, (base, spread) in spreads.items():
        noise = np.random.default_rng([zlib.crc32(name.encode()), seed]).standard_normal(out[name].shape)
        drawn = base * np.exp(spread * noise) if base else spread * noise
        out[name] = jnp.asarray(drawn.astype(out[name].dtype))
    for name, factor in factors.items():
        out[name] = (out[name] * factor).astype(out[name].dtype)
    return out
```

```python
from contextlib import ExitStack

import numpy as np

import concourse.bass as bass
from concourse import mybir

F32 = mybir.dt.float32
BF16 = mybir.dt.bfloat16
I32 = mybir.dt.int32
ALU = mybir.AluOpType
ACT = mybir.ActivationFunctionType
AX = mybir.AxisListType.X

P = 128
BATCH, SEQ, D = 32, 64, 128
TOK = BATCH * SEQ
NT = TOK // P
G = NT // 2
SLOTS = SEQ // 2
E = 8
FF = 512
FC = FF // P
CH = 2
XT = 256
MAX_TILES = (CH * TOK - E) // XT + E
HALVES = XT // P
AHEAD = 3
NCOL = HALVES * (MAX_TILES + AHEAD)
QUAD = D // 4
NEG = -3.0e38
LN_EPS = 1e-5
LOGISTIC_R, LOGISTIC_N = 3.9, 10

_W = [("fwd", 2 * 128), ("alt", 2), ("inv", 2 * 3 * 128), ("wave", 1), ("ident", 128), ("tri", 128),
      ("ones", 128), ("iota", 128), ("pcol", 1), ("choice", CH * NT), ("rev", E), ("steps", E),
      ("reset", E * NT), ("dummy", NCOL), ("dc", 128), ("pick", 3)]
COL, _at = {}, 0
for _name, _n in _W:
    COL[_name] = (_at, _at + _n)
    _at += _n
NCONST = _at

FROM_RE = {(0, 0, 0): (0, 1), (0, 0, 1): (2, 1), (1, 0, 0): (2, -1), (1, 0, 1): (0, 1),
           (0, 1, 0): (1, 1), (0, 1, 1): (3, 1), (1, 1, 0): (3, 1), (1, 1, 1): (1, -1)}
FROM_IM = {(0, 0, 0): (1, -1), (0, 0, 1): (3, -1), (1, 0, 0): (3, -1), (1, 0, 1): (1, 1),
           (0, 1, 0): (0, 1), (0, 1, 1): (2, 1), (1, 1, 0): (2, -1), (1, 1, 1): (0, 1)}


def constants():
    sig = lambda v: 1.0 / (1.0 + np.exp(-v))
    decay, base = 0.1, 0.5
    dop, ser, nor = ((1 - decay) * base + decay * sig(v) for v in (0.7, 0.8, 0.6))
    mem_scale = 0.4 * dop + 0.3 * ser + 0.3 * nor
    c = np.zeros((P, NCONST), np.float64)

    def put(name, v):
        c[:, COL[name][0]:COL[name][1]] = np.asarray(v, np.float64).reshape(P, -1)

    s, k = np.arange(SEQ), np.arange(SLOTS)
    ang = 2 * np.pi * np.outer(s, k) / SEQ
    fwd = np.zeros((P, 2, 2, SLOTS))
    for b in range(2):
        fwd[b * SEQ:(b + 1) * SEQ, 0, b] = np.cos(ang)
        fwd[b * SEQ:(b + 1) * SEQ, 1, b] = -np.sin(ang)
    put("fwd", np.stack([fwd, fwd * mem_scale], 1))
    alt = np.zeros((P, 2))
    for b in range(2):
        alt[b * SEQ:(b + 1) * SEQ, b] = (-1.0) ** s
    put("alt", alt)
    freq = np.arange(SEQ, dtype=np.float64)
    cubed = np.exp(3j * 1.5 * np.arctan(np.log(freq + 1e-10)))
    weight = np.array([cubed[0]] + [cubed[j] + np.conj(cubed[SEQ - j]) for j in range(1, SLOTS)])
    turn = weight[:, None] * np.exp(2j * np.pi * np.outer(k, s) / SEQ) / SEQ / 2
    inv = np.zeros((P, 2, 3, P))
    for b in range(4):
        rows, tile, cols = slice(b * SLOTS, (b + 1) * SLOTS), b // 2, slice((b % 2) * SEQ, (b % 2 + 1) * SEQ)
        inv[rows, tile, 0, cols] = turn.real
        inv[rows, tile, 1, cols] = -turn.imag
        inv[rows, tile, 2, cols] = turn.imag
    put("inv", inv)
    lam = np.arange(SEQ) / SEQ
    alpha = float(np.clip(1.0 * (1.0 + 0.5 * (1.5 - 2.0) / 2.0), 0.1, 3.0))
    beta = 2 * 1 + 1 - 2 * 1.5
    wave = np.sin(alpha * lam) * np.cos(-2.0 * lam + beta * lam ** 2)
    put("wave", np.tile(1.0 + 0.1 * wave, 2))
    put("ident", np.eye(P))
    put("tri", np.triu(np.ones((P, P)), 1))
    put("ones", np.ones((P, P)))
    put("iota", np.tile(np.arange(P), (P, 1)))
    put("pcol", np.arange(P))
    put("choice", np.tile(1 + np.arange(CH * NT), (P, 1)))
    put("rev", np.tile(E - np.arange(E), (P, 1)))
    put("steps", np.tile(XT * np.arange(E), (P, 1)))
    reset = np.ones((P, E, NT))
    reset[:, :, 0] = 0
    put("reset", reset)
    put("dummy", P + CH * TOK + P * np.arange(NCOL)[None, :] + np.arange(P)[:, None])
    put("dc", np.tile(SEQ * (np.arange(P) % SLOTS == 0), (P, 1)))
    put("pick", np.eye(P)[:, :3])
    nyq = np.zeros((BATCH, NT, P))
    for b in range(BATCH):
        nyq[b, b // 2, (b % 2) * SEQ:(b % 2 + 1) * SEQ] = (-1.0) ** s * cubed[SLOTS].real / SEQ / 2
    return c.astype(np.float32), nyq.reshape(BATCH, -1).astype(np.float32), float(mem_scale)


class Steps:

    def __init__(self, eng, sem):
        self.eng, self.sem, self.n, self.base = eng, sem, 0, 0

    def done(self, ins):
        ins.then_inc(self.sem, 1)
        self.n += 1

    def settle(self):
        self.eng.wait_ge(self.sem, self.base + self.n)

    def enter(self, at, per_body):
        self.start, self.per_body = self.n, per_body
        self.base, self.n = self.start + at * per_body, 0

    def leave(self, times):
        assert self.n == self.per_body, (self.n, self.per_body)
        self.base, self.n = 0, self.start + times * self.per_body


def build(nc, x, ctx_in, wq, bq, wk, bk, wv, bv, gate_w, gate_b, w1, b1, w2, b2, cst, nyq, out, mem_scale):
    xn_dram = nc.dram_tensor("xn_rows", [TOK, D], F32, kind="Internal").ap()
    y_rows = CH * TOK + P * NCOL
    y_dram = nc.dram_tensor("y_rows", [y_rows, D], F32, kind="Internal").ap()
    tiles = lambda ap: ap.rearrange("(t p) d -> p t d", p=P)
    x_t, ctx_t, out_t, xn_t = tiles(x), tiles(ctx_in), tiles(out), tiles(xn_dram)

    with ExitStack() as ctx:
        def sb(name, shape, dt=F32):
            return ctx.enter_context(nc.sbuf_tensor(name, shape, dt))

        def sem(name):
            return ctx.enter_context(nc.semaphore(name))

        const = sb("const", [P, NCONST])
        nyq_inv = sb("nyq_inv", [BATCH, NT * P])
        xq = sb("xq", [P, CH, NT, D])
        x_sb, q_sb = xq[:, 0], xq[:, 1]
        ctx_sb = sb("ctx_sb", [P, NT, D])
        x1_sb = sb("x1_sb", [P, NT, D])
        w_raw = sb("w_raw", [P, 3, D])
        basis = sb("basis", [P, 3, 2, 2 * D])
        bias3 = sb("bias3", [3, 3, D])
        bsplit = sb("bsplit", [3, 4, 3 * D])
        bhalf = sb("bhalf", [3, 3, 3 * D], BF16)
        bbasis = sb("bbasis", [3, 3, 2 * D], BF16)
        dc3 = sb("dc3", [3, P], BF16)
        gw_sb = sb("gw_sb", [P, E])
        gb_sb = sb("gb_sb", [P, 1, E])
        w1_sb = sb("w1_sb", [P, E, 2 * FF])
        w2_sb = sb("w2_sb", [P, E * FC, D])
        b1_rows = sb("b1_rows", [E * 2 * FC, P])
        b2_sb = sb("b2_sb", [P, E, D])
        b1_col = sb("b1_col", [P, E * 2 * FC])
        stats = sb("stats", [P, NT, 6])
        tok = sb("tok", [P, 16, NT])
        alt_q = sb("alt_q", [P, NT, 2])
        alt_m = sb("alt_m", [P, NT, 2])
        alt_c = sb("alt_c", [P, 2])
        spec = sb("spec", [P, 2, 2, 2, P])
        spec_n = sb("spec_n", [P, 2, BATCH])
        q_basis = sb("q_basis", [P, 2, 256])
        prod = sb("prod", [P, 4, 256])
        half = sb("half", [P, 4, 128])
        mat = sb("mat", [P, 2, 2, 64])
        mat2 = sb("mat2", [P, 2, 2, 64])
        sums = sb("sums", [P, 2, 256])
        qkv_n = sb("qkv_n", [BATCH, 3, 256])
        prod_n = sb("prod_n", [BATCH, 4, 256])
        half_n = sb("half_n", [BATCH, 4, 128])
        mat_n = sb("mat_n", [BATCH, 2, 2, 64])
        mat2_n = sb("mat2_n", [BATCH, 2, 2, 64])
        sums_n = sb("sums_n", [BATCH, 256])
        xnT = sb("xnT", [P, 2, P])
        logit = sb("logit", [P, NT, E])
        logit2 = sb("logit2", [P, NT, E])
        rt = sb("rt", [P, 6, NT, E])
        hot = sb("hot", [P, CH, NT, E])
        chosen = sb("chosen", [P, E, NT])
        ranks = sb("ranks", [P, E, NT])
        slot_e = sb("slot_e", [P, E, NT])
        ex = sb("ex", [P, 10, E])
        ex2 = sb("ex2", [P, E, E])
        rowsum = sb("rowsum", [P, E], BF16)
        tri_b = sb("tri_b", [P, P], BF16)
        ones_b = sb("ones_b", [P, P], BF16)
        bounds = sb("bounds", [P, 2 * E], I32)
        slot = sb("slot", [P, CH * NT])
        slot_i = sb("slot_i", [P, 3, CH * NT], I32)
        slot_f = sb("slot_f", [P, 2, CH * NT])
        hot_lo = sb("hot_lo", [P, CH * NT, P], BF16)
        hot_hi = sb("hot_hi", [P, CH * NT, NCOL], BF16)
        hot_val = sb("hot_val", [P, CH * NT, 2, NCOL], BF16)
        row = sb("row", [P, 6, NCOL])
        gather_all = sb("gather_all", [P, NCOL], I32)
        scatter_all = sb("scatter_all", [P, NCOL], I32)
        taken = sb("taken", [1, 1])
        gather_now = sb("gather_now", [P, 2, HALVES], I32)
        scatter_now = sb("scatter_now", [P, 2, HALVES], I32)
        xg = sb("xg", [P, 2, HALVES, D])
        xT = sb("xT", [P, XT])
        silu = sb("silu", [P, FC, XT])
        act = sb("act", [P, FC, XT])
        y_sb = sb("y_sb", [P, 2, HALVES, D])
        x_now = sb("x_now", [P, HALVES, D])
        y_in = xq
        res = ctx_sb

        bank = ctx.enter_context(nc.psum_tensor("bank", [P, 8, 512], F32))

        def C(name, rows=P):
            return const[0:rows, COL[name][0]:COL[name][1]]

        const_in, x_in, ctx_in_s, w_in, small_in = (sem(n) for n in ("const_in", "x_in", "ctx_in", "w_in", "small_in"))
        w1_in, w2_in, nyq_in = sem("w1_in"), sem("w2_in"), sem("nyq_in")
        w_turned, basis_ready, bias_ready, b1_turned, b1_ready = (
            sem(n) for n in ("w_turned", "basis_ready", "bias_ready", "b1_turned", "b1_ready"))
        v_step, p_step, a_step = sem("v_step"), sem("p_step"), sem("a_step")
        var_ready, sd_ready, norm2_ready, norm_ready, exp_ready, scale_ready = (
            sem(n) for n in ("var_ready", "sd_ready", "norm2_ready", "norm_ready", "exp_ready", "scale_ready"))
        alt_ready, q_ready, nyq_dft, nyq_spec, nyq_proj, nyq_qkv, nyq_sums = (
            sem(n) for n in ("alt_ready", "q_ready", "nyq_dft", "nyq_spec", "nyq_proj", "nyq_qkv", "nyq_sums"))
        q_basis_ready = sem("q_basis_ready")
        dft_done, spec_ready, proj_done, prod_done, sums_ready, att_done, x1_ready = (
            sem(n) for n in ("dft_done", "spec_ready", "proj_done", "prod_done", "sums_ready", "att_done", "x1_ready"))
        var2_ready, sd2_ready, scale2_ready, xn_ready, xn_out, xn_turned, xnT_ready, gate_done = (
            sem(n) for n in ("var2_ready", "sd2_ready", "scale2_ready", "xn_ready", "xn_out", "xn_turned",
                             "xnT_ready", "gate_done"))
        gap_ready, gap_exp, rowsum_ready, counted, bounds_ready, hots_ready, listed, rows_ready = (
            sem(n) for n in ("gap_ready", "gap_exp", "rowsum_ready", "counted", "bounds_ready", "hots_ready",
                             "listed", "rows_ready"))
        gathered = [[sem(f"gathered{par}{h}") for h in range(HALVES)] for par in range(2)]
        scattered = [[sem(f"scattered{par}{h}") for h in range(HALVES)] for par in range(2)]
        x_moved, xT_turned, xT_ready, up_done, silu_ready, act_ready, down_done, y_ready = (
            sem(n) for n in ("x_moved", "xT_turned", "xT_ready", "up_done", "silu_ready", "act_ready", "down_done", "y_ready"))
        gather_list, scatter_list = sem("gather_list"), sem("scatter_list")
        y_in_s = [sem(f"y_in{c}") for c in range(4)]
        res_ready, out_done = sem("res_ready"), sem("out_done")

        block = ctx.enter_context(nc.Block())

        @block.sync
        def _(sp):
            sp.dma_start(const[:], cst).then_inc(const_in, 16)
            sp.dma_start(x_sb[:], x_t).then_inc(x_in, 16)
            for i, w in enumerate((wq, wk, wv)):
                sp.dma_start(w_raw[:, i, :], w).then_inc(w_in, 16)
            sp.dma_start(w1_sb[:], w1.rearrange("e d h -> d e h")).then_inc(w1_in, 16)
            sp.dma_start(w2_sb[:], w2.rearrange("e (c f) d -> f (e c) d", f=P)).then_inc(w2_in, 16)
            for c in range(4):
                sp.wait_ge(xn_ready, 4 * (c + 1))
                sp.dma_start(xn_t[:, 4 * c:4 * c + 4, :], q_sb[:, 4 * c:4 * c + 4, :]).then_inc(xn_out, 16)
            sp.wait_ge(bounds_ready, 1)
            last = sp.value_load(bounds[0:1, 2 * E - 1:2 * E], min_val=E, max_val=MAX_TILES)
            for h in range(HALVES):
                sp.wait_ge(scattered[0][h], ((last + 1) // 2) * 16 + 16)
                sp.wait_ge(scattered[1][h], (last // 2) * 16 + 32)
            sp.wait_ge(xn_out, 64)
            y_back = y_dram[0:CH * TOK].rearrange("(c t p) d -> p c t d", p=P, c=CH)
            for c in range(4):
                for j in range(CH):
                    sp.dma_start(y_in[:, j, 4 * c:4 * c + 4, :], y_back[:, j, 4 * c:4 * c + 4, :]).then_inc(y_in_s[c], 16)
            for c in range(4):
                sp.wait_ge(res_ready, 4 * (c + 1))
                sp.dma_start(out_t[:, 4 * c:4 * c + 4, :], res[:, 4 * c:4 * c + 4, :]).then_inc(out_done, 16)
            sp.wait_ge(out_done, 64)

        @block.scalar
        def _(a):
            a.dma_start(ctx_sb[:], ctx_t).then_inc(ctx_in_s, 16)
            for i, b in enumerate((bq, bk, bv)):
                a.dma_start(bias3[:, i, :], b.partition_broadcast(3)).then_inc(small_in, 16)
            a.dma_start(b1_rows[:], b1.rearrange("e (c f) -> (e c) f", f=P)).then_inc(small_in, 16)
            a.dma_start(b2_sb[:].rearrange("p e d -> p (e d)"),
                        b2.rearrange("e d -> (e d)").partition_broadcast(P)).then_inc(small_in, 16)
            a.dma_start(gw_sb[:], gate_w).then_inc(small_in, 16)
            a.dma_start(gb_sb[:, 0, :], gate_b.partition_broadcast(P)).then_inc(small_in, 16)
            a.dma_start(nyq_inv[:], nyq).then_inc(nyq_in, 16)
            a.wait_ge(var_ready, 1)
            nc.scalar.activation(tok[:, 3, :], tok[:, 2, :], ACT.Sqrt).then_inc(sd_ready, 1)
            a.wait_ge(norm2_ready, 1)
            nc.scalar.activation(tok[:, 6, :], tok[:, 5, :], ACT.Sqrt).then_inc(norm_ready, 1)
            a.wait_ge(norm_ready, 1)
            nc.scalar.activation(tok[:, 7, :], tok[:, 6, :], ACT.Exp, scale=-1.0).then_inc(exp_ready, 1)
            a.wait_ge(scale_ready, 1)
            with a.Fori(0, NT) as t:
                nc.scalar.activation(q_sb[:, bass.ds(t, 1), :], x_sb[:, bass.ds(t, 1), :], ACT.Identity,
                                     bias=tok[:, 10, bass.ds(t, 1)], scale=tok[:, 9, bass.ds(t, 1)]).then_inc(q_ready, 1)
            a.wait_ge(nyq_dft, 1)
            nc.scalar.activation(spec_n[:], bank[:, 7, 0:2 * BATCH], ACT.Copy).then_inc(nyq_spec, 1)

            def keep_spectra(g, par):
                a.wait_ge(dft_done, g + 1)
                nc.scalar.activation(spec[:, par].rearrange("p s r n -> p (s r n)"), bank[:, par, :],
                                     ACT.Copy).then_inc(spec_ready, 1)

            def keep_q(g, par):
                a.wait_ge(proj_done, g + 1)
                nc.scalar.activation(q_basis[:, par, :], bank[:, 2 + par, 0:256], ACT.Copy).then_inc(q_basis_ready, 1)

            keep_spectra(0, 0)
            a.wait_ge(nyq_proj, 1)
            nc.scalar.activation(qkv_n[:, 0:2, :], bank[0:BATCH, 3, :], ACT.Copy).then_inc(a_step, 1)
            nc.scalar.activation(qkv_n[:, 2, :], bank[0:BATCH, 5, 0:256], ACT.Copy).then_inc(nyq_qkv, 1)
            keep_spectra(1, 1)
            with a.Fori(0, G // 2 - 1) as i:
                for par in range(2):
                    keep_q(2 * i + par, par)
                    keep_spectra(2 * i + 2 + par, par)
            keep_q(G - 2, 0)
            keep_q(G - 1, 1)
            a.wait_ge(var2_ready, 1)
            nc.scalar.activation(tok[:, 3, :], tok[:, 2, :], ACT.Sqrt).then_inc(sd2_ready, 1)
            a.wait_ge(scale2_ready, 1)
            with a.Fori(0, NT) as t:
                nc.scalar.activation(q_sb[:, bass.ds(t, 1), :], x1_sb[:, bass.ds(t, 1), :], ACT.Identity,
                                     bias=tok[:, 10, bass.ds(t, 1)], scale=tok[:, 9, bass.ds(t, 1)]).then_inc(xn_ready, 1)
            a.wait_ge(gap_ready, 1)
            nc.scalar.activation(tok[:, 13, :], tok[:, 12, :], ACT.Exp).then_inc(gap_exp, 1)
            a.wait_ge(bounds_ready, 1)
            a.wait_ge(b1_ready, 1)
            with a.Fori(0, E) as e:
                first = a.value_load(bounds[0:1, bass.ds(e, 1)], min_val=0, max_val=MAX_TILES)
                end = a.value_load(bounds[0:1, bass.ds(e + E, 1)], min_val=1, max_val=MAX_TILES)
                with a.Fori(first, end) as t:
                    for c in range(FC):
                        a.wait_ge(up_done, FC * t + c + 1)
                        nc.scalar.activation(silu[:, c, :], bank[:, c, XT:2 * XT], ACT.Silu,
                                             bias=b1_col[:, bass.ds(e * (2 * FC) + (FC + c), 1)]).then_inc(silu_ready, 1)

        @block.vector
        def _(v):
            st = Steps(v, v_step)

            def op(fn, *args, **kw):
                if st.n:
                    st.settle()
                st.done(fn(*args, **kw))

            tt, ts, stt, cp = nc.vector.tensor_tensor, nc.vector.tensor_scalar, nc.vector.scalar_tensor_tensor, nc.vector.tensor_copy

            v.wait_ge(const_in, 16)
            op(cp, tri_b[:], C("tri"))
            op(cp, ones_b[:], C("ones"))
            op(cp, dc3[:], C("dc", 3))
            def ln_stats(src, ready):
                with v.Fori(0, NT) as t:
                    last = nc.vector.bn_stats(stats[:, bass.ds(t, 1), :], src[:, bass.ds(t, 1), :])
                    st.enter(t, 1)
                    st.done(last)
                    st.leave(NT)

            def ln_moments():
                me, mo, ve, vo = (stats[:, :, j] for j in (1, 4, 2, 5))
                op(tt, tok[:, 0, :], me, mo, ALU.add)
                op(tt, tok[:, 1, :], me, mo, ALU.subtract)
                op(ts, tok[:, 0, :], tok[:, 0, :], 0.5, None, ALU.mult)
                op(tt, tok[:, 1, :], tok[:, 1, :], tok[:, 1, :], ALU.mult)
                op(tt, tok[:, 2, :], ve, vo, ALU.add)
                op(stt, tok[:, 1, :], tok[:, 1, :], D / 4.0, tok[:, 2, :], ALU.mult, ALU.add)
                op(ts, tok[:, 1, :], tok[:, 1, :], 1.0 / D, None, ALU.mult)
                st.settle()
                return ts(tok[:, 2, :], tok[:, 1, :], LN_EPS, None, ALU.add)

            def ln_rstd():
                st.done(nc.vector.reciprocal(tok[:, 4, :], tok[:, 3, :]))
                op(tt, tok[:, 5, :], tok[:, 4, :], tok[:, 4, :], ALU.mult)
                op(tt, tok[:, 5, :], tok[:, 5, :], tok[:, 2, :], ALU.mult)
                op(ts, tok[:, 5, :], tok[:, 5, :], -0.5, 1.5, ALU.mult, ALU.add)
                op(tt, tok[:, 4, :], tok[:, 4, :], tok[:, 5, :], ALU.mult)

            v.wait_ge(x_in, 16)
            ln_stats(x_sb, x_in)
            ln_moments().then_inc(var_ready, 1)
            v.wait_ge(var_ready, 1)
            v.wait_ge(sd_ready, 1)
            ln_rstd()
            op(tt, tok[:, 5, :], tok[:, 4, :], tok[:, 4, :], ALU.mult)
            st.settle()
            stt(tok[:, 5, :], tok[:, 5, :], float(D), tok[:, 1, :], ALU.mult, ALU.mult).then_inc(norm2_ready, 1)
            v.wait_ge(exp_ready, 1)
            op(ts, tok[:, 8, :], tok[:, 7, :], 1.0, None, ALU.add)
            op(nc.vector.reciprocal, tok[:, 8, :], tok[:, 8, :])
            for _ in range(LOGISTIC_N):
                op(ts, tok[:, 7, :], tok[:, 8, :], -1.0, 1.0, ALU.mult, ALU.add)
                op(stt, tok[:, 8, :], tok[:, 8, :], LOGISTIC_R, tok[:, 7, :], ALU.mult, ALU.mult)
            op(ts, tok[:, 8, :], tok[:, 8, :], -0.5, 0.1, ALU.add, ALU.mult)
            op(ts, tok[:, 8, :], tok[:, 8, :], 1.0, C("wave"), ALU.add, ALU.mult)
            op(tt, tok[:, 9, :], tok[:, 8, :], tok[:, 4, :], ALU.mult)
            st.settle()
            stt(tok[:, 10, :], tok[:, 9, :], -1.0, tok[:, 0, :], ALU.mult, ALU.mult).then_inc(scale_ready, 1)
            v.wait_ge(scale_ready, 1)
            alt_b = C("alt").unsqueeze(1).to_broadcast([P, NT, 2])
            tt(alt_q[:], alt_b, tok[:, 9, :].unsqueeze(2).to_broadcast([P, NT, 2]), ALU.mult).then_inc(alt_ready, 1)
            tt(alt_m[:], alt_b, tok[:, 10, :].unsqueeze(2).to_broadcast([P, NT, 2]), ALU.mult).then_inc(alt_ready, 1)
            ts(alt_c[:], C("alt"), mem_scale, None, ALU.mult).then_inc(alt_ready, 1)
            v.wait_ge(w_turned, 1)
            turned = bank[:, 6, 0:3 * D].rearrange("p (s d) -> p s d", s=3)
            for m, table in enumerate((FROM_RE, FROM_IM)):
                for (r, ri, c), (part, sign) in table.items():
                    at = r * 128 + ri * 64 + c * QUAD
                    ts(basis[:, :, m, at:at + QUAD], turned[:, :, part * QUAD:(part + 1) * QUAD],
                       float(sign), None, ALU.mult).then_inc(basis_ready, 1)
            v.wait_ge(small_in, 16 * 7)
            flat = bias3[:, :, :].rearrange("p s d -> p (s d)")
            op(cp, bhalf[:, 0, :], flat)
            op(tt, bsplit[:, 0, :], flat, bhalf[:, 0, :], ALU.subtract)
            op(cp, bhalf[:, 1, :], bsplit[:, 0, :])
            op(tt, bsplit[:, 1, :], bsplit[:, 0, :], bhalf[:, 1, :], ALU.subtract)
            pick = C("pick", 3)
            op(ts, bsplit[:, 2, :], bhalf[:, 0, :], pick[:, 0:1], None, ALU.mult)
            op(stt, bsplit[:, 3, :], bhalf[:, 1, :], pick[:, 1:2], bsplit[:, 2, :], ALU.mult, ALU.add)
            op(stt, bsplit[:, 2, :], bsplit[:, 1, :], pick[:, 2:3], bsplit[:, 3, :], ALU.mult, ALU.add)
            parts = bsplit[:, 2, :].rearrange("p (s d) -> p s d", s=3)
            st.settle()
            for (r, ri, c), (part, sign) in FROM_RE.items():
                at = r * 128 + ri * 64 + c * QUAD
                ts(bbasis[:, :, at:at + QUAD], parts[:, :, part * QUAD:(part + 1) * QUAD], float(sign), None,
                   ALU.mult).then_inc(bias_ready, 1)
            v.wait_ge(b1_turned, 1)
            st.settle()
            cp(b1_col[:], bank[:, 6, 0:E * 2 * FC]).then_inc(b1_ready, 1)

            def hamilton(left, right_of, dst):
                for i in range(2):
                    for qri in range(2):
                        l = left(i, qri).unsqueeze(2).to_broadcast([P, 2, 4, QUAD])
                        r = right_of.rearrange("p (j m c) -> p j m c", j=2, c=QUAD)
                        n = 2 * i + qri
                        o = prod[:, n, :].rearrange("p (j m c) -> p j m c", j=2, c=QUAD)
                        op(tt, o, l, r, ALU.mult)
                op(tt, half[:], prod[:, :, 0:128], prod[:, :, 128:256], ALU.add)
                h = half[:].rearrange("p (i q) n -> p i q n", i=2)
                op(tt, dst[:, :, 0, :], h[:, :, 0, 0:64], h[:, :, 1, 64:128], ALU.subtract)
                op(tt, dst[:, :, 1, :], h[:, :, 0, 64:128], h[:, :, 1, 0:64], ALU.add)

            H_STEPS = 7

            def products(g, par):
                qk = bank[:, 2 + par, :].rearrange("p (s n) -> p s n", s=2)
                left = lambda i, q: q_basis[:, par, :].rearrange(
                    "p (i q j c) -> p i q j c", i=2, q=2, c=QUAD)[:, i, q]
                v.wait_ge(q_basis_ready, g + 1)
                hamilton(left, qk[:, 1, :], mat)
                m = lambda i, q: mat[:, i, q, :].rearrange("p (j c) -> p j c", c=QUAD)
                hamilton(m, bank[:, 4 + par, 0:256], mat2)
                n0 = mat2[:, 0].rearrange("p q (c d) -> p q c d", d=QUAD)
                n1 = mat2[:, 1].rearrange("p q (c d) -> p q c d", d=QUAD)[:, :, ::-1]
                o = sums[:, par, :].rearrange("p (c q s d) -> p s q c d", c=2, q=2, s=2)
                op(tt, o[:, 0], n0, n1, ALU.add)
                st.settle()
                tt(o[:, 1], n0, n1, ALU.subtract).then_inc(sums_ready, 1)

            PRODUCT_STEPS = 2 * H_STEPS + 1

            def residual(g):
                v.wait_ge(att_done, g + 1)
                pair = bass.ds(2 * g, 2)
                tt(x1_sb[:, pair, :], x_sb[:, pair, :], bank[:, 6, 0:256].rearrange("p (t d) -> p t d", t=2),
                   ALU.add).then_inc(x1_ready, 1)
                v.wait_ge(x1_ready, g + 1)
                for j in range(2):
                    st.done(nc.vector.bn_stats(stats[:, bass.ds(2 * g + j, 1), :], x1_sb[:, bass.ds(2 * g + j, 1), :]))

            RESIDUAL_STEPS = 2

            products(0, 0)
            per = 2 * (PRODUCT_STEPS + RESIDUAL_STEPS)
            with v.Fori(0, G // 2 - 1) as i:
                st.enter(i, per)
                for par in (1, 0):
                    g = 2 * i + 1 + (1 - par)
                    products(g, par)
                    residual(g - 1)
                st.leave(G // 2 - 1)
            products(G - 1, 1)
            residual(G - 2)
            residual(G - 1)
            ln_moments().then_inc(var2_ready, 1)
            v.wait_ge(var2_ready, 1)
            v.wait_ge(sd2_ready, 1)
            ln_rstd()
            op(cp, tok[:, 9, :], tok[:, 4, :])
            st.settle()
            stt(tok[:, 10, :], tok[:, 4, :], -1.0, tok[:, 0, :], ALU.mult, ALU.mult).then_inc(scale2_ready, 1)
            for t in range(NT):
                v.wait_ge(xn_turned, t + 1)
                if t >= 2:
                    v.wait_ge(gate_done, t - 1)
                cp(xnT[:, t % 2, :], bank[:, t % 2, 0:P]).then_inc(xnT_ready, 1)

            wide = lambda ap: ap.unsqueeze(2).to_broadcast([P, NT, E])
            rev = C("rev").unsqueeze(1).to_broadcast([P, NT, E])
            v.wait_ge(gate_done, NT)
            op(tt, logit[:], bank[:, 2, 0:NT * E].rearrange("p (t e) -> p t e", e=E), gb_sb[:].to_broadcast([P, NT, E]), ALU.add)

            def choose(src, best, onehot):
                op(nc.vector.tensor_reduce, best, src, AX, ALU.max)
                op(tt, rt[:, 0], src, wide(best), ALU.is_equal)
                op(tt, rt[:, 1], rt[:, 0], rev, ALU.mult)
                op(nc.vector.tensor_reduce, tok[:, 14, :], rt[:, 1], AX, ALU.max)
                op(tt, onehot, rev, wide(tok[:, 14, :]), ALU.is_equal)

            choose(logit[:], tok[:, 11, :], hot[:, 0])
            op(stt, logit2[:], hot[:, 0], NEG, logit[:], ALU.mult, ALU.add)
            choose(logit2[:], tok[:, 15, :], hot[:, 1])
            st.settle()
            tt(tok[:, 12, :], tok[:, 15, :], tok[:, 11, :], ALU.subtract).then_inc(gap_ready, 1)
            by_e = lambda ap: ap.rearrange("p t e -> p e t")
            op(tt, chosen[:], by_e(hot[:, 0]), by_e(hot[:, 1]), ALU.add)
            op(nc.vector.tensor_tensor_scan, ranks[:].rearrange("p e t -> p (e t)"), C("reset"),
               chosen[:].rearrange("p e t -> p (e t)"), 0.0, ALU.mult, ALU.add)
            st.settle()
            cp(rowsum[:], ranks[:, :, NT - 1]).then_inc(rowsum_ready, 1)
            v.wait_ge(counted, 1)
            op(cp, ex[:, 0, :], bank[:, 3, E:2 * E])
            op(tt, ex2[:], ex[:, 0, :].unsqueeze(2).to_broadcast([P, E, E]),
               C("steps").unsqueeze(1).to_broadcast([P, E, E]), ALU.is_gt)
            op(nc.vector.tensor_reduce, ex[:, 1, :], ex2[:], AX, ALU.add)
            op(ts, ex[:, 1, :], ex[:, 1, :], 1.0, None, ALU.max)
            op(nc.vector.tensor_tensor_scan, ex[:, 2, :], C("ones")[:, 0:E], ex[:, 1, :], 0.0, ALU.mult, ALU.add)
            op(tt, ex[:, 3, :], ex[:, 2, :], ex[:, 1, :], ALU.subtract)
            op(cp, bounds[:, 0:E], ex[:, 3, :])
            st.settle()
            cp(bounds[:, E:2 * E], ex[:, 2, :]).then_inc(bounds_ready, 1)
            op(stt, ex[:, 4, :], ex[:, 3, :], float(XT), bank[:, 3, 0:E], ALU.mult, ALU.add)
            op(tt, slot_e[:], ranks[:], chosen[:], ALU.subtract)
            op(tt, slot_e[:], slot_e[:], ex[:, 4, :].unsqueeze(2).to_broadcast([P, E, NT]), ALU.add)
            for j in range(CH):
                op(tt, rt[:, 2 + j], hot[:, j], slot_e[:].rearrange("p e t -> p t e"), ALU.mult)
                op(nc.vector.tensor_reduce, slot[:, j * NT:(j + 1) * NT], rt[:, 2 + j], AX, ALU.add)
            op(cp, slot_i[:, 0, :], slot[:])
            op(ts, slot_i[:, 1, :], slot_i[:, 0, :], 7, None, ALU.logical_shift_right)
            op(ts, slot_i[:, 2, :], slot_i[:, 0, :], P - 1, None, ALU.bitwise_and)
            op(cp, slot_f[:], slot_i[:, 1:3, :])
            shape_lo, shape_hi = [P, CH * NT, P], [P, CH * NT, NCOL]
            op(tt, hot_lo[:], C("iota").unsqueeze(1).to_broadcast(shape_lo),
               slot_f[:, 1, :].unsqueeze(2).to_broadcast(shape_lo), ALU.is_equal)
            op(tt, hot_hi[:], C("iota")[:, 0:NCOL].unsqueeze(1).to_broadcast(shape_hi),
               slot_f[:, 0, :].unsqueeze(2).to_broadcast(shape_hi), ALU.is_equal)
            op(ts, hot_val[:, :, 0, :], hot_hi[:], C("pcol"), None, ALU.mult)
            st.settle()
            tt(hot_val[:, :, 1, :], hot_hi[:], C("choice").unsqueeze(2).to_broadcast(shape_hi), ALU.mult).then_inc(hots_ready, 1)
            v.wait_ge(listed, 1)
            op(cp, row[:, 5, :], bank[:, 7, 0:NCOL])
            op(stt, row[:, 0, :], bank[:, 7, NCOL:2 * NCOL], float(P), row[:, 5, :], ALU.mult, ALU.add)
            op(ts, row[:, 1, :], row[:, 0, :], 0.0, None, ALU.is_equal)
            op(tt, row[:, 2, :], row[:, 1, :], C("dummy"), ALU.mult)
            op(tt, row[:, 2, :], row[:, 2, :], row[:, 0, :], ALU.add)
            op(ts, scatter_all[:], row[:, 2, :], float(-P), None, ALU.add)
            op(ts, row[:, 3, :], row[:, 0, :], float(P + TOK), float(-TOK), ALU.is_ge, ALU.mult)
            op(stt, row[:, 4, :], row[:, 0, :], float(-P), row[:, 3, :], ALU.add, ALU.add)
            st.settle()
            ts(gather_all[:], row[:, 4, :], 0.0, None, ALU.max).then_inc(rows_ready, 1)
            v.wait_ge(gap_exp, 1)
            op(ts, tok[:, 5, :], tok[:, 13, :], 1.0, None, ALU.add)
            op(nc.vector.reciprocal, tok[:, 6, :], tok[:, 5, :])
            op(tt, tok[:, 7, :], tok[:, 13, :], tok[:, 6, :], ALU.mult)

            def keep_xT(n):
                v.wait_ge(xT_turned, n + 1)
                cp(xT[:], bank[:, 4, 0:XT]).then_inc(xT_ready, 1)

            def move_x(n):
                cp(x_now[:], xg[:, bass.ds(n % 2, 1)].rearrange("p o h d -> p (o h) d")).then_inc(x_moved, 1)

            for h in range(HALVES):
                v.wait_ge(gathered[0][h], 16)
            move_x(0)
            keep_xT(0)
            for h in range(HALVES):
                v.wait_ge(gathered[1][h], 16)
            move_x(1)
            with v.Fori(0, E) as e:
                first = v.value_load(bounds[0:1, bass.ds(e, 1)], min_val=0, max_val=MAX_TILES)
                end = v.value_load(bounds[0:1, bass.ds(e + E, 1)], min_val=1, max_val=MAX_TILES)
                with v.Fori(first, end) as t:
                    v.wait_ge(down_done, t + 1)
                    for c in range(FC):
                        v.wait_ge(silu_ready, FC * t + c + 1)
                        stt(act[:, c, :], bank[:, c, 0:XT], b1_col[:, bass.ds(e * (2 * FC) + c, 1)],
                            silu[:, c, :], ALU.add, ALU.mult).then_inc(act_ready, 1)
                    keep_xT(t + 1)
                    v.wait_ge(down_done, t + 2)
                    for h in range(HALVES):
                        v.wait_ge(scattered[0][h], (t // 2) * 16 + 16)
                        v.wait_ge(scattered[1][h], ((t + 1) // 2) * 16 + 16)
                    tt(y_sb[:, bass.ds(t % 2, 1)].rearrange("p o h d -> p (o h) d"), bank[:, 5:7, 0:D],
                       b2_sb[:, bass.ds(e, 1), :].to_broadcast([P, HALVES, D]), ALU.add).then_inc(y_ready, 1)
                    for h in range(HALVES):
                        v.wait_ge(gathered[0][h], (t // 2) * 16 + 32)
                        v.wait_ge(gathered[1][h], ((t + 1) // 2) * 16 + 16)
                    move_x(t + 2)

            for c in range(4):
                v.wait_ge(y_in_s[c], 32)
                for t in range(4 * c, 4 * c + 4):
                    op(stt, res[:, t, :], y_in[:, 0, t, :], tok[:, 6, t:t + 1], x1_sb[:, t, :], ALU.mult, ALU.add)
                    st.settle()
                    stt(res[:, t, :], y_in[:, 1, t, :], tok[:, 7, t:t + 1], res[:, t, :], ALU.mult, ALU.add).then_inc(res_ready, 1)

        @block.gpsimd
        def _(p):
            st = Steps(p, p_step)
            tt = nc.gpsimd.tensor_tensor

            def op(*args):
                if st.n:
                    st.settle()
                st.done(tt(*args))

            def hamilton_n(left, right, dst):
                for i in range(2):
                    for qri in range(2):
                        n = 2 * i + qri
                        for j in range(2):
                            l = left[:, i, qri, j * QUAD:(j + 1) * QUAD].unsqueeze(1).to_broadcast([BATCH, 4, QUAD])
                            op(prod_n[:, n, j * 128:(j + 1) * 128].rearrange("p (m c) -> p m c", c=QUAD), l,
                               right[:, j * 128:(j + 1) * 128].rearrange("p (m c) -> p m c", c=QUAD), ALU.mult)
                op(half_n[:], prod_n[:, :, 0:128], prod_n[:, :, 128:256], ALU.add)
                h = half_n[:].rearrange("p (i q) n -> p i q n", i=2)
                op(dst[:, :, 0, :], h[:, :, 0, 0:64], h[:, :, 1, 64:128], ALU.subtract)
                op(dst[:, :, 1, :], h[:, :, 0, 64:128], h[:, :, 1, 0:64], ALU.add)

            p.wait_ge(a_step, 1)
            p.wait_ge(nyq_qkv, 1)
            hamilton_n(qkv_n[:, 0, :].rearrange("p (i q n) -> p i q n", i=2, q=2), qkv_n[:, 1, :], mat_n)
            hamilton_n(mat_n, qkv_n[:, 2, :], mat2_n)
            n0 = mat2_n[:, 0].rearrange("p q (c d) -> p q c d", d=QUAD)
            n1 = mat2_n[:, 1].rearrange("p q (c d) -> p q c d", d=QUAD)[:, :, ::-1]
            o = sums_n[:].rearrange("p (c q s d) -> p s q c d", c=2, q=2, s=2)
            op(o[:, 0], n0, n1, ALU.add)
            st.settle()
            tt(o[:, 1], n0, n1, ALU.subtract).then_inc(nyq_sums, 1)

            p.wait_ge(rows_ready, 1)
            p.wait_ge(bounds_ready, 1)
            last = p.value_load(bounds[0:1, 2 * E - 1:2 * E], min_val=E, max_val=MAX_TILES)

            def take_waits():
                tt(taken[:], C("pcol", 1), C("pcol", 1), ALU.add)

            def gather(t, par):
                nc.gpsimd.tensor_copy(gather_now[:, par, :], gather_all[:, bass.ds(HALVES * t, HALVES)]).then_inc(gather_list, 1)
                p.wait_ge(gather_list, t + 1)
                take_waits()
                for h in range(HALVES):
                    nc.gpsimd.indirect_dma_start(
                        out=xg[:, par, h, :], out_offset=None, in_=xn_dram,
                        in_offset=bass.IndirectOffsetOnAxis(ap=gather_now[:, par, h:h + 1], axis=0)).then_inc(gathered[par][h], 16)

            def scatter(t, par, pair):
                for h in range(HALVES):
                    p.wait_ge(scattered[par][h], 16 * pair + 16 * (1 + par))
                nc.gpsimd.tensor_copy(scatter_now[:, par, :], scatter_all[:, bass.ds(HALVES * t, HALVES)]).then_inc(scatter_list, 1)
                p.wait_ge(scatter_list, t + 1)
                p.wait_ge(y_ready, t + 2)
                take_waits()
                for h in range(HALVES):
                    nc.gpsimd.indirect_dma_start(
                        out=y_dram, out_offset=bass.IndirectOffsetOnAxis(ap=scatter_now[:, par, h:h + 1], axis=0),
                        in_=y_sb[:, par, h, :], in_offset=None).then_inc(scattered[par][h], 16)

            for n, (par, h) in enumerate((par, h) for par, h in ((0, 0), (0, 1), (1, 0), (1, 1), (1, 0), (1, 1))):
                at = CH * TOK + P * HALVES * MAX_TILES + 32 * n
                p.dma_start(y_dram[at:at + 32], const[0:32, 0:D]).then_inc(scattered[par][h], 16)
            p.wait_ge(xn_out, 64)
            gather(0, 0)
            gather(1, 1)
            p.wait_ge(x_moved, 1)
            gather(2, 0)
            with p.Fori(0, last // 2) as i:
                for par in range(2):
                    t = 2 * i + par
                    p.wait_ge(x_moved, t + 2)
                    gather(t + AHEAD, 1 - par)
                    scatter(t, par, i)
            with p.Fori(last // 2, (last + 1) // 2) as i:
                scatter(2 * i, 0, i)

        @block.tensor
        def _(pe):
            pe.sem_inc(act_ready, FC)
            pe.sem_inc(down_done, 1)
            pe.sem_inc(y_ready, 1)
            mm, tr = nc.tensor.matmul, nc.tensor.transpose
            ident = C("ident")
            pe.wait_ge(const_in, 16)
            pe.wait_ge(w_in, 48)
            for i in range(3):
                last = tr(bank[:, 6, i * D:(i + 1) * D], w_raw[:, i, :], ident)
            last.then_inc(w_turned, 1)
            pe.wait_ge(small_in, 16 * 7)
            pe.wait_ge(alt_ready, 3)
            pe.wait_ge(ctx_in_s, 16)
            pe.wait_ge(x_in, 16)
            for t in range(NT):
                mm(bank[:, 7, 2 * t:2 * t + 2], x_sb[:, t, :], alt_q[:, t, :], start=(t == 0), stop=False,
                   skip_group_check=True)
            mm(bank[:, 7, 0:BATCH], C("ones"), alt_m[:].rearrange("p t b -> p (t b)"), start=False, stop=True,
               skip_group_check=True)
            for t in range(NT):
                last = mm(bank[:, 7, BATCH + 2 * t:BATCH + 2 * t + 2], ctx_sb[:, t, :], alt_c[:], start=True, stop=True,
                          skip_group_check=True)
            last.then_inc(nyq_dft, 1)

            def dft(g):
                if g >= 2:
                    pe.wait_ge(spec_ready, g - 1)
                pe.wait_ge(q_ready, 2 * g + 2)
                y = bank[:, g % 2, :].rearrange("p (s r n) -> p s r n", s=2, r=2)
                for j in range(2):
                    for s, src in enumerate((q_sb, ctx_sb)):
                        last = mm(y[:, s, :, 64 * j:64 * j + 64], src[:, 2 * g + j, :],
                                  C("fwd")[:, 128 * s:128 * s + 128].rearrange("p (r n) -> p r n", r=2), start=True, stop=True)
                last.then_inc(dft_done, 1)

            def project(g):
                pe.wait_ge(spec_ready, g + 1)
                if g >= 2:
                    pe.wait_ge(sums_ready, g - 1)
                par = g % 2
                for i in range(3):
                    dst = bank[:, 2 + par, 256 * i:256 * i + 256] if i < 2 else bank[:, 4 + par, 0:256]
                    src = spec[:, par, min(i, 1)]
                    mm(dst, src[:, 0], basis[:, i, 0, :], start=True, stop=False)
                    mm(dst, src[:, 1], basis[:, i, 1, :], start=False, stop=False)
                    last = mm(dst, dc3[:], bbasis[:, i, :], start=False, stop=True)
                last.then_inc(proj_done, 1)

            def inverse(g):
                pe.wait_ge(sums_ready, g + 1)
                if g >= 1:
                    pe.wait_ge(x1_ready, g)
                s = sums[:, g % 2, :].rearrange("p (n d) -> p n d", d=QUAD)
                sn = sums_n[:].rearrange("p (n d) -> p n d", d=QUAD)
                inv = C("inv").rearrange("p (j m n) -> p j m n", j=2, m=3)
                for j in range(2):
                    o = bank[:, 6, 128 * j:128 * j + 128].rearrange("p (q d) -> p q d", q=4)
                    ny = nyq_inv[:, (2 * g + j) * P:(2 * g + j + 1) * P]
                    mm(o[:, 0:4:2], inv[:, j, 0], s[:, 0:6:5], start=True, stop=False)
                    mm(o[:, 0:4:2], inv[:, j, 1], s[:, 2:8:5], start=False, stop=False)
                    mm(o[:, 0:4:2], ny, sn[:, 0:6:5], start=False, stop=True)
                    mm(o[:, 1:4:2], inv[:, j, 0], s[:, 3:7:3], start=True, stop=False)
                    mm(o[:, 1:4:2], inv[:, j, 2], s[:, 1:5:3], start=False, stop=False)
                    last = mm(o[:, 1:4:2], ny, sn[:, 3:7:3], start=False, stop=True)
                last.then_inc(att_done, 1)

            dft(0)
            dft(1)
            pe.wait_ge(basis_ready, 16)
            pe.wait_ge(nyq_spec, 1)
            for i in range(3):
                dst = bank[0:BATCH, 3, 256 * i:256 * i + 256] if i < 2 else bank[0:BATCH, 5, 0:256]
                last = mm(dst, spec_n[:, min(i, 1), :], basis[:, i, 0, :], start=True, stop=True)
            last.then_inc(nyq_proj, 1)
            tr(bank[:, 6, 0:E * 2 * FC], b1_rows[:], ident[0:E * 2 * FC, 0:E * 2 * FC]).then_inc(b1_turned, 1)
            pe.wait_ge(bias_ready, 8)
            project(0)
            pe.wait_ge(nyq_qkv, 1)
            pe.wait_ge(nyq_in, 16)
            pe.wait_ge(b1_ready, 1)
            for g in range(G):
                if g + 1 < G:
                    project(g + 1)
                if g + 2 < G:
                    dft(g + 2)
                if g == 0:
                    pe.wait_ge(nyq_sums, 1)
                inverse(g)

            for t in range(NT + 1):
                if t < NT:
                    pe.wait_ge(xn_ready, t + 1)
                    if t >= 2:
                        pe.wait_ge(xnT_ready, t - 1)
                    tr(bank[:, t % 2, 0:P], q_sb[:, t, :], ident).then_inc(xn_turned, 1)
                if t >= 1:
                    pe.wait_ge(xnT_ready, t)
                    mm(bank[:, 2, (t - 1) * E:t * E], xnT[:, (t - 1) % 2, :], gw_sb[:], start=True, stop=True).then_inc(gate_done, 1)
            pe.wait_ge(rowsum_ready, 1)
            mm(bank[:, 3, 0:E], tri_b[:], rowsum[:], start=True, stop=True)
            mm(bank[:, 3, E:2 * E], ones_b[:], rowsum[:], start=True, stop=True).then_inc(counted, 1)
            pe.wait_ge(hots_ready, 1)
            for n in range(CH * NT):
                last = mm(bank[:, 7, 0:2 * NCOL], hot_lo[:, n, :], hot_val[:, n].rearrange("p a c -> p (a c)"),
                          start=(n == 0), stop=(n == CH * NT - 1))
            last.then_inc(listed, 1)

            def turn_x():
                for h in range(HALVES):
                    last = tr(bank[:, 4, h * P:(h + 1) * P], x_now[:, h, :], ident)
                last.then_inc(xT_turned, 1)

            pe.wait_ge(x_moved, 1)
            turn_x()
            pe.wait_ge(w1_in, 16)
            pe.wait_ge(w2_in, 16)
            for e in range(E):
                first = pe.value_load(bounds[0:1, e:e + 1], min_val=0, max_val=MAX_TILES)
                end = pe.value_load(bounds[0:1, E + e:E + e + 1], min_val=1, max_val=MAX_TILES)
                with pe.Fori(first, end) as t:
                    pe.wait_ge(xT_ready, t + 1)
                    for c in range(FC):
                        pe.wait_ge(act_ready, FC * t + c + 1)
                        mm(bank[:, c, 0:XT], w1_sb[:, e, c * P:(c + 1) * P], xT[:], start=True, stop=True)
                        mm(bank[:, c, XT:2 * XT], w1_sb[:, e, FF + c * P:FF + (c + 1) * P], xT[:], start=True,
                           stop=True).then_inc(up_done, 1)
                    pe.wait_ge(x_moved, t + 2)
                    turn_x()
                    pe.wait_ge(y_ready, t + 1)
                    for c in range(FC):
                        pe.wait_ge(act_ready, FC * t + FC + c + 1)
                        for h in range(HALVES):
                            last = mm(bank[:, 5 + h, 0:D], act[:, c, h * P:(h + 1) * P], w2_sb[:, e * FC + c, :],
                                      start=(c == 0), stop=(c == FC - 1))
                    last.then_inc(down_done, 1)


_INS = ["x", "ctx_1024", "L0_xattn_Wq", "L0_xattn_bq", "L0_xattn_Wk", "L0_xattn_bk", "L0_xattn_Wv", "L0_xattn_bv",
        "L0_ffn_gate_w", "L0_ffn_gate_b", "L0_ffn_w1", "L0_ffn_b1", "L0_ffn_w2", "L0_ffn_b2"]


def kernel(**inputs):
    import concourse.bacc as bacc
    from concourse.bass_utils import run_bass_kernel_spmd as run

    nc = bacc.Bacc("TRN2", target_bir_lowering=False, num_devices=1)
    arrays, args = {}, []
    for name in _INS:
        arr = np.ascontiguousarray(inputs[name])
        if name in ("x", "ctx_1024"):
            arr = arr.reshape(TOK, D)
        arrays[f"in_{name}"] = arr
        args.append(nc.dram_tensor(f"in_{name}", arr.shape, mybir.dt.from_np(arr.dtype), kind="ExternalInput").ap())
    cst, nyq, mem_scale = constants()
    for name, arr in (("const_table", cst), ("const_nyquist", nyq)):
        arrays[name] = arr
        args.append(nc.dram_tensor(name, arr.shape, F32, kind="ExternalInput").ap())
    out = nc.dram_tensor("out_0", (TOK, D), F32, kind="ExternalOutput").ap()
    build(nc, *args, out, mem_scale)
    r = run(nc, [arrays], core_ids=[0])
    return r.results[0]["out_0"].reshape(BATCH, SEQ, D)
```

```python
from contextlib import ExitStack

import numpy as np

import concourse.bass as bass
from concourse import mybir

F32 = mybir.dt.float32
BF16 = mybir.dt.bfloat16
I32 = mybir.dt.int32
ALU = mybir.AluOpType
ACT = mybir.ActivationFunctionType
AX = mybir.AxisListType.X

P = 128
BATCH, SEQ, D = 32, 64, 128
TOK = BATCH * SEQ
NT = TOK // P
G = NT // 2
SLOTS = SEQ // 2
E = 8
FF = 512
FC = FF // P
CH = 2
XT = 256
MAX_TILES = (CH * TOK - E) // XT + E
HALVES = XT // P
AHEAD = 3
NCOL = HALVES * (MAX_TILES + AHEAD)
QUAD = D // 4
NEG = -3.0e38
LN_EPS = 1e-5
LOGISTIC_R, LOGISTIC_N = 3.9, 10

_W = [("ident", 128), ("fwd", 2 * 128), ("alt", 2 * 2), ("wave", 1), ("dc", 128), ("pick", 3),
      ("inv", 2 * 3 * 128), ("tri", 128), ("ones", 128), ("iota", 128), ("pcol", 1), ("choice", CH * NT),
      ("rev", E), ("steps", E), ("reset", E * NT), ("dummy", NCOL)]
COL, _at = {}, 0
for _name, _n in _W:
    COL[_name] = (_at, _at + _n)
    _at += _n
NCONST = _at
NFIRST = COL["inv"][0]

FROM_RE = {(0, 0, 0): (0, 1), (0, 0, 1): (2, 1), (1, 0, 0): (2, -1), (1, 0, 1): (0, 1),
           (0, 1, 0): (1, 1), (0, 1, 1): (3, 1), (1, 1, 0): (3, 1), (1, 1, 1): (1, -1)}
FROM_IM = {(0, 0, 0): (1, -1), (0, 0, 1): (3, -1), (1, 0, 0): (3, -1), (1, 0, 1): (1, 1),
           (0, 1, 0): (0, 1), (0, 1, 1): (2, 1), (1, 1, 0): (2, -1), (1, 1, 1): (0, 1)}


def constants():
    sig = lambda v: 1.0 / (1.0 + np.exp(-v))
    decay, base = 0.1, 0.5
    dop, ser, nor = ((1 - decay) * base + decay * sig(v) for v in (0.7, 0.8, 0.6))
    mem_scale = 0.4 * dop + 0.3 * ser + 0.3 * nor
    c = np.zeros((P, NCONST), np.float64)

    def put(name, v):
        c[:, COL[name][0]:COL[name][1]] = np.asarray(v, np.float64).reshape(P, -1)

    s, k = np.arange(SEQ), np.arange(SLOTS)
    ang = 2 * np.pi * np.outer(s, k) / SEQ
    fwd = np.zeros((P, 2, 2, SLOTS))
    for b in range(2):
        fwd[b * SEQ:(b + 1) * SEQ, 0, b] = np.cos(ang)
        fwd[b * SEQ:(b + 1) * SEQ, 1, b] = -np.sin(ang)
    put("fwd", np.stack([fwd, fwd * mem_scale], 1))
    alt = np.zeros((P, 2))
    for b in range(2):
        alt[b * SEQ:(b + 1) * SEQ, b] = (-1.0) ** s
    put("alt", np.concatenate([alt, alt * mem_scale], 1))
    freq = np.arange(SEQ, dtype=np.float64)
    cubed = np.exp(3j * 1.5 * np.arctan(np.log(freq + 1e-10)))
    weight = np.array([cubed[0]] + [cubed[j] + np.conj(cubed[SEQ - j]) for j in range(1, SLOTS)])
    turn = weight[:, None] * np.exp(2j * np.pi * np.outer(k, s) / SEQ) / SEQ / 2
    inv = np.zeros((P, 2, 3, P))
    for b in range(4):
        rows, tile, cols = slice(b * SLOTS, (b + 1) * SLOTS), b // 2, slice((b % 2) * SEQ, (b % 2 + 1) * SEQ)
        inv[rows, tile, 0, cols] = turn.real
        inv[rows, tile, 1, cols] = -turn.imag
        inv[rows, tile, 2, cols] = turn.imag
    put("inv", inv)
    lam = np.arange(SEQ) / SEQ
    alpha = float(np.clip(1.0 * (1.0 + 0.5 * (1.5 - 2.0) / 2.0), 0.1, 3.0))
    beta = 2 * 1 + 1 - 2 * 1.5
    wave = np.sin(alpha * lam) * np.cos(-2.0 * lam + beta * lam ** 2)
    put("wave", np.tile(1.0 + 0.1 * wave, 2))
    put("ident", np.eye(P))
    put("tri", np.triu(np.ones((P, P)), 1))
    put("ones", np.ones((P, P)))
    put("iota", np.tile(np.arange(P), (P, 1)))
    put("pcol", np.arange(P))
    put("choice", np.tile(1 + np.arange(CH * NT), (P, 1)))
    put("rev", np.tile(E - np.arange(E), (P, 1)))
    put("steps", np.tile(XT * np.arange(E), (P, 1)))
    reset = np.ones((P, E, NT))
    reset[:, :, 0] = 0
    put("reset", reset)
    put("dummy", P + CH * TOK + P * np.arange(NCOL)[None, :] + np.arange(P)[:, None])
    put("dc", np.tile(SEQ * (np.arange(P) % SLOTS == 0), (P, 1)))
    put("pick", np.eye(P)[:, :3])
    nyq = np.zeros((BATCH, NT, P))
    for b in range(BATCH):
        nyq[b, b // 2, (b % 2) * SEQ:(b % 2 + 1) * SEQ] = (-1.0) ** s * cubed[SLOTS].real / SEQ / 2
    return c.astype(np.float32), nyq.reshape(BATCH, -1).astype(np.float32), float(mem_scale)


class Steps:

    def __init__(self, eng, sem):
        self.eng, self.sem, self.n, self.base = eng, sem, 0, 0

    def done(self, ins):
        ins.then_inc(self.sem, 1)
        self.n += 1

    def settle(self):
        self.eng.wait_ge(self.sem, self.base + self.n)

    def enter(self, at, per_body):
        self.start, self.per_body = self.n, per_body
        self.base, self.n = self.start + at * per_body, 0

    def leave(self, times):
        assert self.n == self.per_body, (self.n, self.per_body)
        self.base, self.n = 0, self.start + times * self.per_body


def build(nc, x, ctx_in, wq, bq, wk, bk, wv, bv, gate_w, gate_b, w1, b1, w2, b2, cst, nyq, out, mem_scale):
    xn_dram = nc.dram_tensor("xn_rows", [TOK, D], F32, kind="Internal").ap()
    y_rows = CH * TOK + P * NCOL
    y_dram = nc.dram_tensor("y_rows", [y_rows, D], F32, kind="Internal").ap()
    tiles = lambda ap: ap.rearrange("(t p) d -> p t d", p=P)
    x_t, ctx_t, out_t, xn_t = tiles(x), tiles(ctx_in), tiles(out), tiles(xn_dram)

    with ExitStack() as ctx:
        def sb(name, shape, dt=F32):
            return ctx.enter_context(nc.sbuf_tensor(name, shape, dt))

        def sem(name):
            return ctx.enter_context(nc.semaphore(name))

        const = sb("const", [P, NCONST])
        nyq_inv = sb("nyq_inv", [BATCH, NT * P])
        xq = sb("xq", [P, CH, NT, D])
        x_sb, q_sb = xq[:, 0], xq[:, 1]
        ctx_sb = sb("ctx_sb", [P, NT, D])
        x1_sb = sb("x1_sb", [P, NT, D])
        w_raw = sb("w_raw", [P, 3, D])
        basis = sb("basis", [P, 3, 2, 2 * D])
        bias3 = sb("bias3", [3, 3, D])
        bsplit = sb("bsplit", [3, 4, 3 * D])
        bhalf = sb("bhalf", [3, 3, 3 * D], BF16)
        bbasis = sb("bbasis", [3, 3, 2 * D], BF16)
        dc3 = sb("dc3", [3, P], BF16)
        gw_sb = sb("gw_sb", [P, E])
        gb_sb = sb("gb_sb", [P, 1, E])
        w1_sb = sb("w1_sb", [P, E, 2 * FF])
        w2_sb = sb("w2_sb", [P, E * FC, D])
        b1_rows = sb("b1_rows", [E * 2 * FC, P])
        b2_sb = sb("b2_sb", [P, E, D])
        b1_col = sb("b1_col", [P, E * 2 * FC])
        stats = sb("stats", [P, NT, 6])
        tok = sb("tok", [P, 16, NT])
        spec = sb("spec", [P, 2, 2, 2, P])
        spec_n = sb("spec_n", [P, 2, BATCH])
        q_basis = sb("q_basis", [P, 2, 256])
        prod1 = sb("prod1", [P, 4, 256])
        half1 = sb("half1", [P, 4, 128])
        prod2 = sb("prod2", [P, 4, 256])
        half2 = sb("half2", [P, 4, 128])
        mat = sb("mat", [P, 2, 2, 64])
        mat2 = sb("mat2", [P, 2, 2, 64])
        sums = sb("sums", [P, 2, 14 * QUAD])
        q_n = sb("q_n", [BATCH, 256])
        prod_n = sb("prod_n", [BATCH, 4, 256])
        half_n = sb("half_n", [BATCH, 4, 128])
        mat_n = sb("mat_n", [BATCH, 2, 2, 64])
        mat2_n = sb("mat2_n", [BATCH, 2, 2, 64])
        sums_n = sb("sums_n", [BATCH, 14 * QUAD])
        logit = sb("logit", [P, NT, E])
        logit2 = sb("logit2", [P, NT, E])
        rt = sb("rt", [P, 6, NT, E])
        hot = sb("hot", [P, CH, NT, E])
        chosen = sb("chosen", [P, E, NT])
        ranks = sb("ranks", [P, E, NT])
        slot_e = sb("slot_e", [P, E, NT])
        ex = sb("ex", [P, 10, E])
        ex2 = sb("ex2", [P, E, E])
        rowsum = sb("rowsum", [P, E], BF16)
        tri_b = sb("tri_b", [P, P], BF16)
        ones_b = sb("ones_b", [P, P], BF16)
        bounds = sb("bounds", [P, 2 * E], I32)
        slot = sb("slot", [P, CH * NT])
        slot_i = sb("slot_i", [P, 3, CH * NT], I32)
        slot_f = sb("slot_f", [P, 2, CH * NT], BF16)
        iota_b = sb("iota_b", [P, P], BF16)
        choice_b = sb("choice_b", [P, CH * NT], BF16)
        hot_lo = sb("hot_lo", [P, CH * NT, P], BF16)
        hot_hi = sb("hot_hi", [P, CH * NT, NCOL], BF16)
        hot_val = sb("hot_val", [P, CH * NT, 2, NCOL], BF16)
        row = sb("row", [P, 6, NCOL])
        gather_all = sb("gather_all", [P, NCOL], I32)
        scatter_all = sb("scatter_all", [P, NCOL], I32)
        taken, taken_a = sb("taken", [1, 1]), sb("taken_a", [1, 1])
        gather_now = sb("gather_now", [P, 2, HALVES], I32)
        scatter_now = sb("scatter_now", [P, 2, HALVES], I32)
        xg = sb("xg", [P, 2, HALVES, D])
        xT = sb("xT", [P, XT])
        silu = sb("silu", [P, FC, XT])
        act = sb("act", [P, FC, XT])
        y_sb = sb("y_sb", [P, 2, HALVES, D])
        x_now = sb("x_now", [P, HALVES, D])
        y_in = xq
        xnT = res = ctx_sb

        bank = ctx.enter_context(nc.psum_tensor("bank", [P, 8, 512], F32))

        def C(name, rows=P):
            return const[0:rows, COL[name][0]:COL[name][1]]

        def sums_from(m2, s):
            n0 = m2[:, 0].rearrange("p q (c d) -> p q c d", d=QUAD)
            n1 = m2[:, 1].rearrange("p q (c d) -> p q c d", d=QUAD)
            add = s.rearrange("p (q r d) -> p q r d", q=2, d=QUAD)[:, :, 0:5:4]
            sub = s[:, 3 * QUAD:9 * QUAD].rearrange("p (q r d) -> p q r d", q=2, d=QUAD)[:, :, 0:3:2]
            return (add, n0[:, :, ::-1], n1), (sub, n0[:, ::-1, ::-1], n1[:, ::-1])

        const_in, rest_in, ctx_in_s, w_in, small_in = (sem(n) for n in ("const_in", "rest_in", "ctx_in", "w_in", "small_in"))
        x_in = [sem(f"x_in{c}") for c in range(2)]
        bias_in, b1_in = sem("bias_in"), sem("b1_in")
        w1_in, w2_in, nyq_in = sem("w1_in"), sem("w2_in"), sem("nyq_in")
        w_turned, basis_ready, parts_ready, bias_ready, b1_turned, b1_ready = (
            sem(n) for n in ("w_turned", "basis_ready", "parts_ready", "bias_ready", "b1_turned", "b1_ready"))
        v_step, p_step, a_step = sem("v_step"), sem("p_step"), sem("a_step")
        var_ready, sd_ready, norm_ready, exp_ready, scale_ready = (
            sem(n) for n in ("var_ready", "sd_ready", "norm_ready", "exp_ready", "scale_ready"))
        q_ready, nyq_dft, nyq_spec, nyq_proj, nyq_q, nyq_prod, nyq_half, nyq_sums = (
            sem(n) for n in ("q_ready", "nyq_dft", "nyq_spec", "nyq_proj", "nyq_q", "nyq_prod", "nyq_half", "nyq_sums"))
        q_basis_ready = sem("q_basis_ready")
        dft_done, spec_ready, proj_done, prod1_ready, half1_ready, prod2_ready, half2_ready, sums_ready, att_done, x1_ready = (
            sem(n) for n in ("dft_done", "spec_ready", "proj_done", "prod1_ready", "half1_ready", "prod2_ready",
                             "half2_ready", "sums_ready", "att_done", "x1_ready"))
        var2_ready, sd2_ready, scale2_ready, xn_ready, xn_out, xn_turned, xnT_first, xnT_ready, gate_done = (
            sem(n) for n in ("var2_ready", "sd2_ready", "scale2_ready", "xn_ready", "xn_out", "xn_turned",
                             "xnT_first", "xnT_ready", "gate_done"))
        gap_ready, gap_exp, rowsum_ready, counted, bounds_ready, hot_hi_ready, hot_p_ready, hots_ready, listed, rows_ready = (
            sem(n) for n in ("gap_ready", "gap_exp", "rowsum_ready", "counted", "bounds_ready", "hot_hi_ready", "hot_p_ready", "hots_ready",
                             "listed", "rows_ready"))
        gathered = [[sem(f"gathered{par}{h}") for h in range(HALVES)] for par in range(2)]
        scattered = [[sem(f"scattered{par}{h}") for h in range(HALVES)] for par in range(2)]
        x_moved, xT_turned, xT_ready, up_done, silu_ready, act_ready, down_done, y_ready = (
            sem(n) for n in ("x_moved", "xT_turned", "xT_ready", "up_done", "silu_ready", "act_ready", "down_done", "y_ready"))
        gather_list, scatter_list = sem("gather_list"), sem("scatter_list")
        y_in_s = [sem(f"y_in{c}") for c in range(4)]
        p_ready, second_ready, res_ready, out_done = (sem(n) for n in ("p_ready", "second_ready", "res_ready", "out_done"))

        block = ctx.enter_context(nc.Block())

        @block.sync
        def _(sp):
            for c in range(2):
                sp.dma_start(x_sb[:, 8 * c:8 * c + 8, :], x_t[:, 8 * c:8 * c + 8, :]).then_inc(x_in[c], 16)
            sp.dma_start(ctx_sb[:], ctx_t).then_inc(ctx_in_s, 16)
            sp.dma_start(const[:, NFIRST:], cst[:, NFIRST:]).then_inc(rest_in, 16)
            sp.dma_start(nyq_inv[:], nyq).then_inc(nyq_in, 16)
            sp.wait_ge(small_in, 48)
            sp.dma_start(w1_sb[:], w1.rearrange("e d h -> d e h")).then_inc(w1_in, 16)
            sp.dma_start(w2_sb[:], w2.rearrange("e (c f) d -> f (e c) d", f=P)).then_inc(w2_in, 16)
            for c in range(4):
                sp.wait_ge(xn_ready, 4 * (c + 1))
                sp.dma_start(xn_t[:, 4 * c:4 * c + 4, :], q_sb[:, 4 * c:4 * c + 4, :]).then_inc(xn_out, 16)
            sp.wait_ge(bounds_ready, 1)
            last = sp.value_load(bounds[0:1, 2 * E - 1:2 * E], min_val=E, max_val=MAX_TILES)
            for h in range(HALVES):
                sp.wait_ge(scattered[0][h], ((last + 1) // 2) * 16 + 16)
                sp.wait_ge(scattered[1][h], (last // 2) * 16 + 32)
            sp.wait_ge(xn_out, 64)
            y_back = y_dram[0:CH * TOK].rearrange("(c t p) d -> p c t d", p=P, c=CH)
            for c in range(4):
                for j in range(CH):
                    sp.dma_start(y_in[:, j, 4 * c:4 * c + 4, :], y_back[:, j, 4 * c:4 * c + 4, :]).then_inc(y_in_s[c], 16)
            for c in range(4):
                sp.wait_ge(res_ready, c + 1)
                sp.dma_start(out_t[:, 4 * c:4 * c + 4, :], res[:, 4 * c:4 * c + 4, :]).then_inc(out_done, 16)
            sp.wait_ge(out_done, 64)

        @block.scalar
        def _(a):
            a.dma_start(const[:, 0:NFIRST], cst[:, 0:NFIRST]).then_inc(const_in, 16)
            for i, b in enumerate((bq, bk, bv)):
                a.dma_start(bias3[:, i, :], b.partition_broadcast(3)).then_inc(bias_in, 16)
            for i, w in enumerate((wq, wk, wv)):
                a.dma_start(w_raw[:, i, :], w).then_inc(w_in, 16)
            a.dma_start(b1_rows[:], b1.rearrange("e (c f) -> (e c) f", f=P)).then_inc(b1_in, 16)
            a.dma_start(b2_sb[:].rearrange("p e d -> p (e d)"),
                        b2.rearrange("e d -> (e d)").partition_broadcast(P)).then_inc(small_in, 16)
            a.dma_start(gw_sb[:], gate_w).then_inc(small_in, 16)
            a.dma_start(gb_sb[:, 0, :], gate_b.partition_broadcast(P)).then_inc(small_in, 16)
            a.wait_ge(w_turned, 1)
            turned = bank[:, 6, 0:3 * D].rearrange("p (s d) -> p s d", s=3)

            def to_basis(m, table):
                for (r, ri, c), (part, sign) in table.items():
                    at = r * 128 + ri * 64 + c * QUAD
                    nc.scalar.activation(basis[:, :, m, at:at + QUAD], turned[:, :, part * QUAD:(part + 1) * QUAD],
                                         ACT.Copy, scale=float(sign)).then_inc(basis_ready, 1)

            to_basis(0, FROM_RE)
            a.wait_ge(var_ready, 1)
            nc.scalar.activation(tok[:, 3, :], tok[:, 2, :], ACT.Sqrt).then_inc(sd_ready, 1)
            nc.scalar.activation(tok[:, 6, :], tok[:, 1, :], ACT.Sqrt, scale=float(D)).then_inc(sd_ready, 1)
            nc.scalar.activation(taken_a[:], C("wave", 1), ACT.Exp)
            a.wait_ge(norm_ready, 1)
            nc.scalar.activation(tok[:, 7, :], tok[:, 5, :], ACT.Exp, scale=-1.0).then_inc(exp_ready, 1)
            to_basis(1, FROM_IM)
            a.wait_ge(scale_ready, 1)
            def normalise(tiles):
                for t in tiles:
                    nc.scalar.activation(q_sb[:, t, :], x_sb[:, t, :], ACT.Identity,
                                         bias=tok[:, 10, t:t + 1], scale=tok[:, 9, t:t + 1]).then_inc(q_ready, 1)

            def keep_spectra(g, par):
                a.wait_ge(dft_done, g + 1)
                nc.scalar.activation(spec[:, par].rearrange("p s r n -> p (s r n)"), bank[:, par, :],
                                     ACT.Copy).then_inc(spec_ready, 1)

            def keep_q(g, par):
                a.wait_ge(proj_done, g + 1)
                nc.scalar.activation(q_basis[:, par, :], bank[:, 2 + par, 0:256], ACT.Copy).then_inc(q_basis_ready, 1)

            normalise(range(0, 4))
            keep_spectra(0, 0)
            normalise(range(4, 8))
            keep_spectra(1, 1)
            keep_q(0, 0)
            normalise(range(8, 12))
            keep_q(1, 1)
            normalise(range(12, NT))
            keep_spectra(2, 0)
            a.wait_ge(nyq_dft, 1)
            nc.scalar.activation(spec_n[:], bank[:, 7, 0:2 * BATCH], ACT.Copy).then_inc(nyq_spec, 1)
            a.wait_ge(nyq_proj, 1)
            nc.scalar.activation(q_n[:], bank[0:BATCH, 6, 0:256], ACT.Copy).then_inc(nyq_q, 1)
            with a.Fori(1, G // 2 - 1) as i:
                for par in range(2):
                    keep_q(2 * i + par, par)
                    keep_spectra(2 * i + par + 1, 1 - par)
            keep_q(G - 2, 0)
            keep_spectra(G - 1, 1)
            keep_q(G - 1, 1)
            for n, part in enumerate((range(0, NT - 4), range(NT - 4, NT))):
                at = slice(part[0], part[-1] + 1)
                a.wait_ge(var2_ready, n + 1)
                nc.scalar.activation(tok[:, 3, at], tok[:, 2, at], ACT.Sqrt).then_inc(sd2_ready, 1)
                if n == 1:
                    for b in range(2):
                        a.wait_ge(xn_turned, b + 1)
                        nc.scalar.activation(xnT[:, 4 * b:4 * b + 4, :].rearrange("p t n -> p (t n)"), bank[:, b, :],
                                             ACT.Copy).then_inc(xnT_first, 1)
                a.wait_ge(scale2_ready, n + 1)
                for t in part:
                    nc.scalar.activation(q_sb[:, t, :], x1_sb[:, t, :], ACT.Identity,
                                         bias=tok[:, 10, t:t + 1], scale=tok[:, 4, t:t + 1]).then_inc(xn_ready, 1)
            a.wait_ge(gap_ready, 1)
            nc.scalar.activation(tok[:, 13, :], tok[:, 12, :], ACT.Exp).then_inc(gap_exp, 1)
            for j in range(CH):
                n = slice(j * NT, (j + 1) * NT)
                a.wait_ge(hot_hi_ready, j + 1)
                nc.scalar.activation(hot_val[:, n, 0, :], hot_hi[:, n], ACT.Copy, scale=C("pcol")).then_inc(hot_p_ready, 1)
            nc.scalar.activation(taken_a[:], C("pcol", 1), ACT.Silu)
            a.wait_ge(bounds_ready, 1)
            a.wait_ge(b1_ready, 1)
            with a.Fori(0, E) as e:
                first = a.value_load(bounds[0:1, bass.ds(e, 1)], min_val=0, max_val=MAX_TILES)
                end = a.value_load(bounds[0:1, bass.ds(e + E, 1)], min_val=1, max_val=MAX_TILES)
                with a.Fori(first, end) as t:
                    for c in range(FC):
                        a.wait_ge(up_done, FC * t + c + 1)
                        nc.scalar.activation(silu[:, c, :], bank[:, c, XT:2 * XT], ACT.Silu,
                                             bias=b1_col[:, bass.ds(e * (2 * FC) + (FC + c), 1)]).then_inc(silu_ready, 1)
            a.wait_ge(p_ready, 1)
            for c in range(4):
                a.wait_ge(y_in_s[c], 32)
                for t in range(4 * c, 4 * c + 4):
                    nc.scalar.activation(y_in[:, 1, t, :], y_in[:, 1, t, :], ACT.Copy,
                                         scale=tok[:, 7, t:t + 1]).then_inc(second_ready, 1)

        @block.vector
        def _(v):
            st = Steps(v, v_step)

            def op(fn, *args, **kw):
                if st.n:
                    st.settle()
                st.done(fn(*args, **kw))

            tt, ts, stt, cp = nc.vector.tensor_tensor, nc.vector.tensor_scalar, nc.vector.scalar_tensor_tensor, nc.vector.tensor_copy

            def ln_moments(part):
                me, mo, ve, vo = (stats[:, part, j] for j in (1, 4, 2, 5))
                st.done(tt(tok[:, 0, part], me, mo, ALU.add))
                st.done(tt(tok[:, 1, part], me, mo, ALU.subtract))
                st.done(tt(tok[:, 2, part], ve, vo, ALU.add))
                st.settle()
                st.done(ts(tok[:, 0, part], tok[:, 0, part], 0.5, None, ALU.mult))
                st.done(tt(tok[:, 1, part], tok[:, 1, part], tok[:, 1, part], ALU.mult))
                op(stt, tok[:, 1, part], tok[:, 1, part], D / 4.0, tok[:, 2, part], ALU.mult, ALU.add)
                st.settle()
                st.done(ts(tok[:, 2, part], tok[:, 1, part], 1.0 / D, LN_EPS, ALU.mult, ALU.add))
                return ts(tok[:, 1, part], tok[:, 1, part], 1.0 / D, None, ALU.mult)

            def ln_rstd(part):
                st.done(nc.vector.reciprocal(tok[:, 4, part], tok[:, 3, part]))
                op(tt, tok[:, 5, part], tok[:, 4, part], tok[:, 4, part], ALU.mult)
                op(tt, tok[:, 5, part], tok[:, 5, part], tok[:, 2, part], ALU.mult)
                op(ts, tok[:, 5, part], tok[:, 5, part], -0.5, 1.5, ALU.mult, ALU.add)
                op(tt, tok[:, 4, part], tok[:, 4, part], tok[:, 5, part], ALU.mult)

            every = slice(0, NT)
            for c in range(2):
                v.wait_ge(x_in[c], 16)
                for t in range(8 * c, 8 * c + 8):
                    st.done(nc.vector.bn_stats(stats[:, t, :], x_sb[:, t, :]))
            st.settle()
            ln_moments(every).then_inc(var_ready, 1)
            v.wait_ge(const_in, 16)
            st.done(cp(dc3[:], C("dc", 3)))
            v.wait_ge(var_ready, 1)
            v.wait_ge(sd_ready, 2)
            ln_rstd(every)
            st.settle()
            tt(tok[:, 5, :], tok[:, 4, :], tok[:, 6, :], ALU.mult).then_inc(norm_ready, 1)
            v.wait_ge(parts_ready, 1)
            parts = bsplit[:, 2, :].rearrange("p (s d) -> p s d", s=3)
            for (r, ri, c), (part, sign) in FROM_RE.items():
                at = r * 128 + ri * 64 + c * QUAD
                ts(bbasis[:, :, at:at + QUAD], parts[:, :, part * QUAD:(part + 1) * QUAD], float(sign), None,
                   ALU.mult).then_inc(bias_ready, 1)
            v.wait_ge(exp_ready, 1)
            op(ts, tok[:, 8, :], tok[:, 7, :], 1.0, None, ALU.add)
            op(nc.vector.reciprocal, tok[:, 8, :], tok[:, 8, :])
            for _ in range(LOGISTIC_N):
                op(ts, tok[:, 7, :], tok[:, 8, :], -1.0, 1.0, ALU.mult, ALU.add)
                op(stt, tok[:, 8, :], tok[:, 8, :], LOGISTIC_R, tok[:, 7, :], ALU.mult, ALU.mult)
            op(ts, tok[:, 8, :], tok[:, 8, :], 0.1, 0.95, ALU.mult, ALU.add)
            op(stt, tok[:, 9, :], tok[:, 8, :], C("wave"), tok[:, 4, :], ALU.mult, ALU.mult)
            st.settle()
            stt(tok[:, 10, :], tok[:, 9, :], -1.0, tok[:, 0, :], ALU.mult, ALU.mult).then_inc(scale_ready, 1)
            v.wait_ge(b1_turned, 1)
            cp(b1_col[:], bank[:, 5, 0:E * 2 * FC]).then_inc(b1_ready, 1)
            v.wait_ge(rest_in, 16)
            st.done(cp(tri_b[:], C("tri")))
            st.done(cp(ones_b[:], C("ones")))
            st.done(cp(iota_b[:], C("iota")))
            st.done(cp(choice_b[:], C("choice")))

            def multiply(left, right_of, prod, rows=P):
                for i in range(2):
                    for qri in range(2):
                        l = left(i, qri).unsqueeze(2).to_broadcast([rows, 2, 4, QUAD])
                        r = right_of.rearrange("p (j m c) -> p j m c", j=2, c=QUAD)
                        o = prod[:, 2 * i + qri, :].rearrange("p (j m c) -> p j m c", j=2, c=QUAD)
                        last = tt(o, l, r, ALU.mult)
                return last

            def combine(half, dst):
                h = half[:].rearrange("p (i q) n -> p i q n", i=2)
                st.done(tt(dst[:, :, 0, :], h[:, :, 0, 0:64], h[:, :, 1, 64:128], ALU.subtract))
                st.done(tt(dst[:, :, 1, :], h[:, :, 0, 64:128], h[:, :, 1, 0:64], ALU.add))

            def residual(g, par):
                v.wait_ge(att_done, g + 1)
                pair = bass.ds(2 * g, 2)
                tt(x1_sb[:, pair, :], x_sb[:, pair, :], bank[:, 6 + par, 0:256].rearrange("p (t d) -> p t d", t=2),
                   ALU.add).then_inc(x1_ready, 1)

            def residual_stats(g):
                v.wait_ge(x1_ready, g + 1)
                for j in range(2):
                    st.done(nc.vector.bn_stats(stats[:, bass.ds(2 * g + j, 1), :], x1_sb[:, bass.ds(2 * g + j, 1), :]))

            def finish(g, par):
                v.wait_ge(half2_ready, g + 1)
                combine(half2, mat2)

            def finish_sums(g, par):
                (o, n0, n1), (o2, m0, m1) = sums_from(mat2, sums[:, par])
                tt(o, n0, n1, ALU.add)
                tt(o2, m0, m1, ALU.subtract).then_inc(sums_ready, 1)

            def stage(g, par, residuals, has_before=True, beside=None):
                qk = bank[:, 2 + par, :].rearrange("p (s n) -> p s n", s=2)
                left = lambda i, q: q_basis[:, par, :].rearrange(
                    "p (i q j c) -> p i q j c", i=2, q=2, c=QUAD)[:, i, q]
                v.wait_ge(q_basis_ready, g + 1)
                multiply(left, qk[:, 1, :], prod1).then_inc(prod1_ready, 1)
                if has_before:
                    finish(g - 1, 1 - par)
                for r, p in residuals:
                    residual(r, p)
                if has_before:
                    st.settle()
                    finish_sums(g - 1, 1 - par)
                if beside:
                    beside()
                v.wait_ge(half1_ready, g + 1)
                combine(half1, mat)
                for r, p in residuals:
                    residual_stats(r)
                st.settle()
                m = lambda i, q: mat[:, i, q, :].rearrange("p (j c) -> p j c", c=QUAD)
                multiply(m, bank[:, 4 + par, 0:256], prod2).then_inc(prod2_ready, 1)

            STAGE_STEPS = 2 + 2 + 2

            stage(0, 0, [], has_before=False)
            stage(1, 1, [])
            by_row = lambda ap: ap.rearrange("p (i q j c) -> p i q j c", i=2, q=2, c=QUAD)
            v.wait_ge(nyq_q, 1)
            multiply(lambda i, q: by_row(q_n[:])[:, i, q], bank[0:BATCH, 6, 256:512], prod_n, BATCH).then_inc(nyq_prod, 1)

            def nyquist_v():
                v.wait_ge(nyq_half, 1)
                combine(half_n, mat_n)
                st.settle()
                multiply(lambda i, q: mat_n[:, i, q, :].rearrange("p (j c) -> p j c", c=QUAD),
                         bank[0:BATCH, 7, 128:384], prod_n, BATCH).then_inc(nyq_prod, 1)

            stage(2, 0, [], beside=nyquist_v)
            v.wait_ge(nyq_half, 2)
            combine(half_n, mat2_n)
            st.settle()
            (o, n0, n1), (o2, m0, m1) = sums_from(mat2_n, sums_n)
            tt(o, n0, n1, ALU.add)
            tt(o2, m0, m1, ALU.subtract).then_inc(nyq_sums, 1)
            stage(3, 1, [(0, 0), (1, 1)])
            with v.Fori(2, G // 2) as i:
                st.enter(i - 2, 2 * STAGE_STEPS)
                for par in range(2):
                    g = 2 * i + par
                    stage(g, par, [(g - 2, par)])
                st.leave(G // 2 - 2)
            first = slice(0, NT - 4)
            rest = slice(NT - 4, NT)
            st.settle()
            ln_moments(first).then_inc(var2_ready, 1)
            finish(G - 1, 1)
            st.settle()
            finish_sums(G - 1, 1)

            def scale2(part, n):
                v.wait_ge(var2_ready, n)
                v.wait_ge(sd2_ready, n)
                ln_rstd(part)
                st.settle()
                stt(tok[:, 10, part], tok[:, 4, part], -1.0, tok[:, 0, part], ALU.mult, ALU.mult).then_inc(scale2_ready, 1)

            scale2(first, 1)
            residual(G - 2, 0)
            residual_stats(G - 2)
            residual(G - 1, 1)
            residual_stats(G - 1)
            st.settle()
            ln_moments(rest).then_inc(var2_ready, 1)
            scale2(rest, 2)
            for b in range(2, NT // 4):
                v.wait_ge(xn_turned, b + 1)
                cp(xnT[:, 4 * b:4 * b + 4, :].rearrange("p t n -> p (t n)"), bank[:, b, :]).then_inc(xnT_ready, 1)

            wide = lambda ap: ap.unsqueeze(2).to_broadcast([P, NT, E])
            rev = C("rev").unsqueeze(1).to_broadcast([P, NT, E])
            v.wait_ge(gate_done, NT)
            v.wait_ge(small_in, 48)
            op(tt, logit[:], bank[:, 4, 0:NT * E].rearrange("p (t e) -> p t e", e=E), gb_sb[:].to_broadcast([P, NT, E]), ALU.add)

            def choose(src, best, onehot):
                op(nc.vector.tensor_reduce, best, src, AX, ALU.max)
                op(tt, rt[:, 0], src, wide(best), ALU.is_equal)
                op(tt, rt[:, 1], rt[:, 0], rev, ALU.mult)
                op(nc.vector.tensor_reduce, tok[:, 14, :], rt[:, 1], AX, ALU.max)
                op(tt, onehot, rev, wide(tok[:, 14, :]), ALU.is_equal)

            choose(logit[:], tok[:, 11, :], hot[:, 0])
            op(stt, logit2[:], hot[:, 0], NEG, logit[:], ALU.mult, ALU.add)
            choose(logit2[:], tok[:, 15, :], hot[:, 1])
            st.settle()
            tt(tok[:, 12, :], tok[:, 15, :], tok[:, 11, :], ALU.subtract).then_inc(gap_ready, 1)
            by_e = lambda ap: ap.rearrange("p t e -> p e t")
            op(tt, chosen[:], by_e(hot[:, 0]), by_e(hot[:, 1]), ALU.add)
            op(nc.vector.tensor_tensor_scan, ranks[:].rearrange("p e t -> p (e t)"), C("reset"),
               chosen[:].rearrange("p e t -> p (e t)"), 0.0, ALU.mult, ALU.add)
            st.settle()
            cp(rowsum[:], ranks[:, :, NT - 1]).then_inc(rowsum_ready, 1)
            v.wait_ge(counted, 1)
            op(cp, ex[:, 0, :], bank[:, 3, E:2 * E])
            op(tt, ex2[:], ex[:, 0, :].unsqueeze(2).to_broadcast([P, E, E]),
               C("steps").unsqueeze(1).to_broadcast([P, E, E]), ALU.is_gt)
            op(nc.vector.tensor_reduce, ex[:, 1, :], ex2[:], AX, ALU.add)
            op(ts, ex[:, 1, :], ex[:, 1, :], 1.0, None, ALU.max)
            op(nc.vector.tensor_tensor_scan, ex[:, 2, :], C("ones")[:, 0:E], ex[:, 1, :], 0.0, ALU.mult, ALU.add)
            op(tt, ex[:, 3, :], ex[:, 2, :], ex[:, 1, :], ALU.subtract)
            op(cp, bounds[:, 0:E], ex[:, 3, :])
            st.settle()
            cp(bounds[:, E:2 * E], ex[:, 2, :]).then_inc(bounds_ready, 1)
            op(stt, ex[:, 4, :], ex[:, 3, :], float(XT), bank[:, 3, 0:E], ALU.mult, ALU.add)
            op(tt, slot_e[:], ranks[:], chosen[:], ALU.subtract)
            op(tt, slot_e[:], slot_e[:], ex[:, 4, :].unsqueeze(2).to_broadcast([P, E, NT]), ALU.add)
            for j in range(CH):
                op(tt, rt[:, 2 + j], hot[:, j], slot_e[:].rearrange("p e t -> p t e"), ALU.mult)
                op(nc.vector.tensor_reduce, slot[:, j * NT:(j + 1) * NT], rt[:, 2 + j], AX, ALU.add)
            op(cp, slot_i[:, 0, :], slot[:])
            op(ts, slot_i[:, 1, :], slot_i[:, 0, :], 7, None, ALU.logical_shift_right)
            op(ts, slot_i[:, 2, :], slot_i[:, 0, :], P - 1, None, ALU.bitwise_and)
            op(cp, slot_f[:], slot_i[:, 1:3, :])
            for j in range(CH):
                n = slice(j * NT, (j + 1) * NT)
                shape_lo, shape_hi = [P, NT, P], [P, NT, NCOL]
                if j == 0:
                    st.settle()
                tt(hot_hi[:, n], iota_b[:, 0:NCOL].unsqueeze(1).to_broadcast(shape_hi),
                   slot_f[:, 0, n].unsqueeze(2).to_broadcast(shape_hi), ALU.is_equal).then_inc(hot_hi_ready, 1)
                st.done(tt(hot_lo[:, n], iota_b[:].unsqueeze(1).to_broadcast(shape_lo),
                           slot_f[:, 1, n].unsqueeze(2).to_broadcast(shape_lo), ALU.is_equal))
                v.wait_ge(hot_hi_ready, j + 1)
                tt(hot_val[:, n, 1, :], hot_hi[:, n], choice_b[:, n].unsqueeze(2).to_broadcast(shape_hi),
                   ALU.mult).then_inc(hots_ready, 1)
            v.wait_ge(listed, 1)
            op(cp, row[:, 5, :], bank[:, 7, 0:NCOL])
            op(stt, row[:, 0, :], bank[:, 7, NCOL:2 * NCOL], float(P), row[:, 5, :], ALU.mult, ALU.add)
            op(ts, row[:, 1, :], row[:, 0, :], 0.0, None, ALU.is_equal)
            op(tt, row[:, 2, :], row[:, 1, :], C("dummy"), ALU.mult)
            op(tt, row[:, 2, :], row[:, 2, :], row[:, 0, :], ALU.add)
            op(ts, scatter_all[:], row[:, 2, :], float(-P), None, ALU.add)
            op(ts, row[:, 3, :], row[:, 0, :], float(P + TOK), float(-TOK), ALU.is_ge, ALU.mult)
            op(stt, row[:, 4, :], row[:, 0, :], float(-P), row[:, 3, :], ALU.add, ALU.add)
            st.settle()
            ts(gather_all[:], row[:, 4, :], 0.0, None, ALU.max).then_inc(rows_ready, 1)
            v.wait_ge(gap_exp, 1)
            op(ts, tok[:, 5, :], tok[:, 13, :], 1.0, None, ALU.add)
            op(nc.vector.reciprocal, tok[:, 6, :], tok[:, 5, :])
            st.settle()
            tt(tok[:, 7, :], tok[:, 13, :], tok[:, 6, :], ALU.mult).then_inc(p_ready, 1)

            def keep_xT(n):
                v.wait_ge(xT_turned, n + 1)
                cp(xT[:], bank[:, 4, 0:XT]).then_inc(xT_ready, 1)

            def move_x(n):
                cp(x_now[:], xg[:, bass.ds(n % 2, 1)].rearrange("p o h d -> p (o h) d")).then_inc(x_moved, 1)

            for h in range(HALVES):
                v.wait_ge(gathered[0][h], 16)
            move_x(0)
            keep_xT(0)
            for h in range(HALVES):
                v.wait_ge(gathered[1][h], 16)
            move_x(1)
            with v.Fori(0, E) as e:
                first = v.value_load(bounds[0:1, bass.ds(e, 1)], min_val=0, max_val=MAX_TILES)
                end = v.value_load(bounds[0:1, bass.ds(e + E, 1)], min_val=1, max_val=MAX_TILES)
                with v.Fori(first, end) as t:
                    v.wait_ge(down_done, t + 1)
                    for c in range(FC):
                        v.wait_ge(silu_ready, FC * t + c + 1)
                        stt(act[:, c, :], bank[:, c, 0:XT], b1_col[:, bass.ds(e * (2 * FC) + c, 1)],
                            silu[:, c, :], ALU.add, ALU.mult).then_inc(act_ready, 1)
                    keep_xT(t + 1)
                    v.wait_ge(down_done, t + 2)
                    for h in range(HALVES):
                        v.wait_ge(scattered[0][h], (t // 2) * 16 + 16)
                        v.wait_ge(scattered[1][h], ((t + 1) // 2) * 16 + 16)
                    tt(y_sb[:, bass.ds(t % 2, 1)].rearrange("p o h d -> p (o h) d"), bank[:, 5:7, 0:D],
                       b2_sb[:, bass.ds(e, 1), :].to_broadcast([P, HALVES, D]), ALU.add).then_inc(y_ready, 1)
                    for h in range(HALVES):
                        v.wait_ge(gathered[0][h], (t // 2) * 16 + 32)
                        v.wait_ge(gathered[1][h], ((t + 1) // 2) * 16 + 16)
                    move_x(t + 2)

            st.settle()
            for c in range(4):
                v.wait_ge(y_in_s[c], 32)
                four = slice(4 * c, 4 * c + 4)
                for t in range(4 * c, 4 * c + 4):
                    st.done(stt(res[:, t, :], y_in[:, 0, t, :], tok[:, 6, t:t + 1], x1_sb[:, t, :], ALU.mult, ALU.add))
                st.settle()
                v.wait_ge(second_ready, 4 * c + 4)
                tt(res[:, four, :], res[:, four, :], y_in[:, 1, four, :], ALU.add).then_inc(res_ready, 1)

        @block.gpsimd
        def _(p):
            st = Steps(p, p_step)
            tt = nc.gpsimd.tensor_tensor

            p.wait_ge(bias_in, 48)
            p.wait_ge(const_in, 16)
            flat = bias3[:, :, :].rearrange("p s d -> p (s d)")
            copy = nc.gpsimd.tensor_copy
            pick = lambda i: C("pick", 3)[:, i:i + 1].to_broadcast([3, 3 * D])

            def chain(fn, *args):
                if st.n:
                    st.settle()
                st.done(fn(*args))

            chain(copy, bhalf[:, 0, :], flat)
            chain(tt, bsplit[:, 0, :], flat, bhalf[:, 0, :], ALU.subtract)
            chain(copy, bhalf[:, 1, :], bsplit[:, 0, :])
            chain(tt, bsplit[:, 1, :], bsplit[:, 0, :], bhalf[:, 1, :], ALU.subtract)
            chain(tt, bsplit[:, 0, :], bhalf[:, 0, :], pick(0), ALU.mult)
            chain(tt, bsplit[:, 2, :], bhalf[:, 1, :], pick(1), ALU.mult)
            chain(tt, bsplit[:, 3, :], bsplit[:, 1, :], pick(2), ALU.mult)
            chain(tt, bsplit[:, 0, :], bsplit[:, 0, :], bsplit[:, 2, :], ALU.add)
            st.settle()
            tt(bsplit[:, 2, :], bsplit[:, 0, :], bsplit[:, 3, :], ALU.add).then_inc(parts_ready, 1)

            def add_halves(g):
                p.wait_ge(prod1_ready, g + 1)
                tt(half1[:], prod1[:, :, 0:128], prod1[:, :, 128:256], ALU.add).then_inc(half1_ready, 1)
                p.wait_ge(prod2_ready, g + 1)
                tt(half2[:], prod2[:, :, 0:128], prod2[:, :, 128:256], ALU.add).then_inc(half2_ready, 1)

            add_halves(0)
            add_halves(1)
            p.wait_ge(nyq_prod, 1)
            tt(half_n[:], prod_n[:, :, 0:128], prod_n[:, :, 128:256], ALU.add).then_inc(nyq_half, 1)
            p.wait_ge(prod1_ready, 3)
            tt(half1[:], prod1[:, :, 0:128], prod1[:, :, 128:256], ALU.add).then_inc(half1_ready, 1)
            p.wait_ge(nyq_prod, 2)
            tt(half_n[:], prod_n[:, :, 0:128], prod_n[:, :, 128:256], ALU.add).then_inc(nyq_half, 1)
            p.wait_ge(prod2_ready, 3)
            tt(half2[:], prod2[:, :, 0:128], prod2[:, :, 128:256], ALU.add).then_inc(half2_ready, 1)
            with p.Fori(3, G) as g:
                add_halves(g)

            for n, (par, h) in enumerate((par, h) for par, h in ((0, 0), (0, 1), (1, 0), (1, 1), (1, 0), (1, 1))):
                at = CH * TOK + P * HALVES * MAX_TILES + 32 * n
                p.dma_start(y_dram[at:at + 32], const[0:32, 0:D]).then_inc(scattered[par][h], 16)

            p.wait_ge(rows_ready, 1)
            p.wait_ge(bounds_ready, 1)
            last = p.value_load(bounds[0:1, 2 * E - 1:2 * E], min_val=E, max_val=MAX_TILES)

            def take_waits():
                tt(taken[:], C("pcol", 1), C("pcol", 1), ALU.add)

            def gather(t, par):
                nc.gpsimd.tensor_copy(gather_now[:, par, :], gather_all[:, bass.ds(HALVES * t, HALVES)]).then_inc(gather_list, 1)
                p.wait_ge(gather_list, t + 1)
                take_waits()
                for h in range(HALVES):
                    nc.gpsimd.indirect_dma_start(
                        out=xg[:, par, h, :], out_offset=None, in_=xn_dram,
                        in_offset=bass.IndirectOffsetOnAxis(ap=gather_now[:, par, h:h + 1], axis=0)).then_inc(gathered[par][h], 16)

            def scatter(t, par, pair):
                for h in range(HALVES):
                    p.wait_ge(scattered[par][h], 16 * pair + 16 * (1 + par))
                nc.gpsimd.tensor_copy(scatter_now[:, par, :], scatter_all[:, bass.ds(HALVES * t, HALVES)]).then_inc(scatter_list, 1)
                p.wait_ge(scatter_list, t + 1)
                p.wait_ge(y_ready, t + 2)
                take_waits()
                for h in range(HALVES):
                    nc.gpsimd.indirect_dma_start(
                        out=y_dram, out_offset=bass.IndirectOffsetOnAxis(ap=scatter_now[:, par, h:h + 1], axis=0),
                        in_=y_sb[:, par, h, :], in_offset=None).then_inc(scattered[par][h], 16)

            p.wait_ge(xn_out, 64)
            gather(0, 0)
            gather(1, 1)
            p.wait_ge(x_moved, 1)
            gather(2, 0)
            with p.Fori(0, last // 2) as i:
                for par in range(2):
                    t = 2 * i + par
                    p.wait_ge(x_moved, t + 2)
                    gather(t + AHEAD, 1 - par)
                    scatter(t, par, i)
            with p.If(last % 2 == 1):
                scatter(last - 1, 0, last // 2)

        @block.tensor
        def _(pe):
            pe.sem_inc(act_ready, FC)
            pe.sem_inc(down_done, 1)
            pe.sem_inc(y_ready, 1)
            mm, tr = nc.tensor.matmul, nc.tensor.transpose
            ident = C("ident")
            pe.wait_ge(const_in, 16)
            pe.wait_ge(w_in, 48)
            for i in range(3):
                last = tr(bank[:, 6, i * D:(i + 1) * D], w_raw[:, i, :], ident)
            last.then_inc(w_turned, 1)
            pe.wait_ge(b1_in, 16)
            tr(bank[:, 5, 0:E * 2 * FC], b1_rows[:], ident[0:E * 2 * FC, 0:E * 2 * FC]).then_inc(b1_turned, 1)

            def nyquist(s, src):
                for t in range(NT):
                    last = mm(bank[:, 7, s * BATCH + 2 * t:s * BATCH + 2 * t + 2], src[:, t, :],
                              C("alt")[:, 2 * s:2 * s + 2], start=True, stop=True, skip_group_check=True)
                return last

            pe.wait_ge(ctx_in_s, 16)
            pe.wait_ge(bias_ready, 8)
            nyquist(1, ctx_sb)

            def dft(g):
                if g >= 2:
                    pe.wait_ge(spec_ready, g - 1)
                y = bank[:, g % 2, :].rearrange("p (s r n) -> p s r n", s=2, r=2)
                for s, src in ((1, ctx_sb), (0, q_sb)):
                    if s == 0:
                        pe.wait_ge(q_ready, 2 * g + 2)
                    for j in range(2):
                        last = mm(y[:, s, :, 64 * j:64 * j + 64], src[:, 2 * g + j, :],
                                  C("fwd")[:, 128 * s:128 * s + 128].rearrange("p (r n) -> p r n", r=2), start=True, stop=True)
                last.then_inc(dft_done, 1)

            def project(g):
                pe.wait_ge(spec_ready, g + 1)
                if g >= 2:
                    pe.wait_ge(prod2_ready, g - 1)
                par = g % 2
                for i in range(3):
                    dst = bank[:, 2 + par, 256 * i:256 * i + 256] if i < 2 else bank[:, 4 + par, 0:256]
                    src = spec[:, par, min(i, 1)]
                    mm(dst, src[:, 0], basis[:, i, 0, :], start=True, stop=False)
                    mm(dst, src[:, 1], basis[:, i, 1, :], start=False, stop=False)
                    last = mm(dst, dc3[:], bbasis[:, i, :], start=False, stop=True)
                last.then_inc(proj_done, 1)

            def inverse(g):
                pe.wait_ge(sums_ready, g + 1)
                if g >= 2:
                    pe.wait_ge(x1_ready, g - 1)
                s = sums[:, g % 2, :].rearrange("p (n d) -> p n d", d=QUAD)
                inv = C("inv").rearrange("p (j m n) -> p j m n", j=2, m=3)
                for j in range(2):
                    at = bank[:, 6 + g % 2, 128 * j:128 * j + 128]
                    o = at.rearrange("p (q d) -> p q d", q=4)
                    mm(at, inv[:, j, 0], sums[:, g % 2, 4 * QUAD:8 * QUAD], start=True, stop=False, skip_group_check=True)
                    mm(o[:, 0:3:2], inv[:, j, 1], s[:, 3:12:8][:, ::-1], start=False, stop=False, skip_group_check=True)
                    mm(o[:, 1:4:2], inv[:, j, 2], s[:, 0:9:8][:, ::-1], start=False, stop=False, skip_group_check=True)
                    last = mm(at, nyq_inv[:, (2 * g + j) * P:(2 * g + j + 1) * P], sums_n[:, 4 * QUAD:8 * QUAD],
                              start=False, stop=True, skip_group_check=True)
                last.then_inc(att_done, 1)

            dft(0)
            pe.wait_ge(basis_ready, 16)
            project(0)
            dft(1)
            pe.wait_ge(b1_ready, 1)
            project(1)
            dft(2)
            pe.wait_ge(q_ready, NT)
            nyquist(0, q_sb).then_inc(nyq_dft, 1)
            pe.wait_ge(nyq_spec, 1)
            for i in range(3):
                dst = bank[0:BATCH, 6, 256 * i:256 * i + 256] if i < 2 else bank[0:BATCH, 7, 128:384]
                last = mm(dst, spec_n[:, min(i, 1), :], basis[:, i, 0, :], start=True, stop=True)
            last.then_inc(nyq_proj, 1)
            pe.wait_ge(rest_in, 16)
            pe.wait_ge(nyq_in, 16)
            for g in range(1, G):
                if g + 1 < G:
                    project(g + 1)
                if g + 2 < G:
                    dft(g + 2)
                if g == 2:
                    pe.wait_ge(nyq_sums, 1)
                    inverse(0)
                if g >= 2:
                    inverse(g - 1)
            inverse(G - 1)

            pe.wait_ge(small_in, 48)
            pe.wait_ge(prod2_ready, G)
            def turn_xn(tiles):
                for t in tiles:
                    pe.wait_ge(xn_ready, t + 1)
                    last = tr(bank[:, t // 4, (t % 4) * P:(t % 4 + 1) * P], q_sb[:, t, :], ident)
                    if t % 4 == 3:
                        last.then_inc(xn_turned, 1)

            def gate(tiles):
                for t in tiles:
                    if t < NT // 2:
                        pe.wait_ge(xnT_first, t // 4 + 1)
                    else:
                        pe.wait_ge(xnT_ready, t // 4 - 1)
                    mm(bank[:, 4, t * E:(t + 1) * E], xnT[:, t, :], gw_sb[:], start=True, stop=True).then_inc(gate_done, 1)

            turn_xn(range(0, 12))
            gate(range(0, 4))
            turn_xn(range(12, NT))
            gate(range(4, NT))
            pe.wait_ge(rowsum_ready, 1)
            mm(bank[:, 3, 0:E], tri_b[:], rowsum[:], start=True, stop=True)
            mm(bank[:, 3, E:2 * E], ones_b[:], rowsum[:], start=True, stop=True).then_inc(counted, 1)
            for n in range(CH * NT):
                if n % NT == 0:
                    pe.wait_ge(hots_ready, n // NT + 1)
                    pe.wait_ge(hot_p_ready, n // NT + 1)
                last = mm(bank[:, 7, 0:2 * NCOL], hot_lo[:, n, :], hot_val[:, n].rearrange("p a c -> p (a c)"),
                          start=(n == 0), stop=(n == CH * NT - 1))
            last.then_inc(listed, 1)

            def turn_x():
                for h in range(HALVES):
                    last = tr(bank[:, 4, h * P:(h + 1) * P], x_now[:, h, :], ident)
                last.then_inc(xT_turned, 1)

            pe.wait_ge(x_moved, 1)
            turn_x()
            pe.wait_ge(w1_in, 16)
            pe.wait_ge(w2_in, 16)
            for e in range(E):
                first = pe.value_load(bounds[0:1, e:e + 1], min_val=0, max_val=MAX_TILES)
                end = pe.value_load(bounds[0:1, E + e:E + e + 1], min_val=1, max_val=MAX_TILES)
                with pe.Fori(first, end) as t:
                    pe.wait_ge(xT_ready, t + 1)
                    for c in range(FC):
                        pe.wait_ge(act_ready, FC * t + c + 1)
                        mm(bank[:, c, 0:XT], w1_sb[:, e, c * P:(c + 1) * P], xT[:], start=True, stop=True)
                        mm(bank[:, c, XT:2 * XT], w1_sb[:, e, FF + c * P:FF + (c + 1) * P], xT[:], start=True,
                           stop=True).then_inc(up_done, 1)
                    pe.wait_ge(x_moved, t + 2)
                    turn_x()
                    pe.wait_ge(y_ready, t + 1)
                    for c in range(FC):
                        pe.wait_ge(act_ready, FC * t + FC + c + 1)
                        for h in range(HALVES):
                            last = mm(bank[:, 5 + h, 0:D], act[:, c, h * P:(h + 1) * P], w2_sb[:, e * FC + c, :],
                                      start=(c == 0), stop=(c == FC - 1))
                    last.then_inc(down_done, 1)


_INS = ["x", "ctx_1024", "L0_xattn_Wq", "L0_xattn_bq", "L0_xattn_Wk", "L0_xattn_bk", "L0_xattn_Wv", "L0_xattn_bv",
        "L0_ffn_gate_w", "L0_ffn_gate_b", "L0_ffn_w1", "L0_ffn_b1", "L0_ffn_w2", "L0_ffn_b2"]


def kernel(**inputs):
    import concourse.bacc as bacc
    from concourse.bass_utils import run_bass_kernel_spmd as run

    nc = bacc.Bacc("TRN2", target_bir_lowering=False, num_devices=1)
    arrays, args = {}, []
    for name in _INS:
        arr = np.ascontiguousarray(inputs[name])
        if name in ("x", "ctx_1024"):
            arr = arr.reshape(TOK, D)
        arrays[f"in_{name}"] = arr
        args.append(nc.dram_tensor(f"in_{name}", arr.shape, mybir.dt.from_np(arr.dtype), kind="ExternalInput").ap())
    cst, nyq, mem_scale = constants()
    for name, arr in (("const_table", cst), ("const_nyquist", nyq)):
        arrays[name] = arr
        args.append(nc.dram_tensor(name, arr.shape, F32, kind="ExternalInput").ap())
    out = nc.dram_tensor("out_0", (TOK, D), F32, kind="ExternalOutput").ap()
    build(nc, *args, out, mem_scale)
    r = run(nc, [arrays], core_ids=[0])
    return r.results[0]["out_0"].reshape(BATCH, SEQ, D)
```

```python
from contextlib import ExitStack

import numpy as np

import concourse.bass as bass
from concourse import mybir

F32 = mybir.dt.float32
F32R = mybir.dt.float32r
BF16 = mybir.dt.bfloat16
I32 = mybir.dt.int32
ALU = mybir.AluOpType
ACT = mybir.ActivationFunctionType
AX = mybir.AxisListType.X

P = 128
BATCH, SEQ, D = 32, 64, 128
TOK = BATCH * SEQ
NT = TOK // P
G = NT // 2
SLOTS = SEQ // 2
E = 8
FF = 512
FC = FF // P
CH = 2
XT = 256
MAX_TILES = (CH * TOK - E) // XT + E
HALVES = XT // P
AHEAD = 3
NCOL = HALVES * (MAX_TILES + AHEAD)
HOT_STARTS = (0, NT // 2, NT, CH * NT - NT // 2, CH * NT - NT // 4)
HOT_PARTS = tuple(zip(HOT_STARTS, HOT_STARTS[1:] + (CH * NT,)))
QUAD = D // 4
NEG = -3.0e38
LN_EPS = 1e-5
LOGISTIC_R, LOGISTIC_N = 3.9, 10

_W = [("ident", 128), ("fwd", 2 * 128), ("alt", 2 * 2), ("wave", 1), ("dc", 128), ("pick", 3),
      ("inv", 2 * 3 * 128), ("tri", 128), ("ones", 128), ("iota", 128), ("pcol", 1), ("choice", CH * NT),
      ("rev", E), ("steps", E), ("reset", E * NT), ("dummy", NCOL)]
COL, _at = {}, 0
for _name, _n in _W:
    COL[_name] = (_at, _at + _n)
    _at += _n
NCONST = _at
NFIRST = COL["inv"][0]

FROM_RE = {(0, 0, 0): (0, 1), (0, 0, 1): (2, 1), (1, 0, 0): (2, -1), (1, 0, 1): (0, 1),
           (0, 1, 0): (1, 1), (0, 1, 1): (3, 1), (1, 1, 0): (3, 1), (1, 1, 1): (1, -1)}
FROM_IM = {(0, 0, 0): (1, -1), (0, 0, 1): (3, -1), (1, 0, 0): (3, -1), (1, 0, 1): (1, 1),
           (0, 1, 0): (0, 1), (0, 1, 1): (2, 1), (1, 1, 0): (2, -1), (1, 1, 1): (0, 1)}


def constants():
    sig = lambda v: 1.0 / (1.0 + np.exp(-v))
    decay, base = 0.1, 0.5
    dop, ser, nor = ((1 - decay) * base + decay * sig(v) for v in (0.7, 0.8, 0.6))
    mem_scale = 0.4 * dop + 0.3 * ser + 0.3 * nor
    c = np.zeros((P, NCONST), np.float64)

    def put(name, v):
        c[:, COL[name][0]:COL[name][1]] = np.asarray(v, np.float64).reshape(P, -1)

    s, k = np.arange(SEQ), np.arange(SLOTS)
    ang = 2 * np.pi * np.outer(s, k) / SEQ
    fwd = np.zeros((P, 2, 2, SLOTS))
    for b in range(2):
        fwd[b * SEQ:(b + 1) * SEQ, 0, b] = np.cos(ang)
        fwd[b * SEQ:(b + 1) * SEQ, 1, b] = -np.sin(ang)
    put("fwd", np.stack([fwd, fwd * mem_scale], 1))
    alt = np.zeros((P, 2))
    for b in range(2):
        alt[b * SEQ:(b + 1) * SEQ, b] = (-1.0) ** s
    put("alt", np.concatenate([alt, alt * mem_scale], 1))
    freq = np.arange(SEQ, dtype=np.float64)
    cubed = np.exp(3j * 1.5 * np.arctan(np.log(freq + 1e-10)))
    weight = np.array([cubed[0]] + [cubed[j] + np.conj(cubed[SEQ - j]) for j in range(1, SLOTS)])
    turn = weight[:, None] * np.exp(2j * np.pi * np.outer(k, s) / SEQ) / SEQ / 2
    inv = np.zeros((P, 2, 3, P))
    for b in range(4):
        rows, tile, cols = slice(b * SLOTS, (b + 1) * SLOTS), b // 2, slice((b % 2) * SEQ, (b % 2 + 1) * SEQ)
        inv[rows, tile, 0, cols] = turn.real
        inv[rows, tile, 1, cols] = -turn.imag
        inv[rows, tile, 2, cols] = turn.imag
    put("inv", inv)
    lam = np.arange(SEQ) / SEQ
    alpha = float(np.clip(1.0 * (1.0 + 0.5 * (1.5 - 2.0) / 2.0), 0.1, 3.0))
    beta = 2 * 1 + 1 - 2 * 1.5
    wave = np.sin(alpha * lam) * np.cos(-2.0 * lam + beta * lam ** 2)
    put("wave", np.tile(1.0 + 0.1 * wave, 2))
    put("ident", np.eye(P))
    put("tri", np.triu(np.ones((P, P)), 1))
    put("ones", np.ones((P, P)))
    put("iota", np.tile(np.arange(P), (P, 1)))
    put("pcol", np.arange(P))
    put("choice", np.tile(1 + np.arange(CH * NT), (P, 1)))
    put("rev", np.tile(E - np.arange(E), (P, 1)))
    put("steps", np.tile(XT * np.arange(E), (P, 1)))
    reset = np.ones((P, E, NT))
    reset[:, :, 0] = 0
    put("reset", reset)
    put("dummy", P + CH * TOK + P * np.arange(NCOL)[None, :] + np.arange(P)[:, None])
    put("dc", np.tile(SEQ * (np.arange(P) % SLOTS == 0), (P, 1)))
    put("pick", np.eye(P)[:, :3])
    nyq = np.zeros((BATCH, NT, P))
    for b in range(BATCH):
        nyq[b, b // 2, (b % 2) * SEQ:(b % 2 + 1) * SEQ] = (-1.0) ** s * cubed[SLOTS].real / SEQ / 2
    return c.astype(np.float32), nyq.reshape(BATCH, -1).astype(np.float32), float(mem_scale)


class Steps:

    def __init__(self, eng, sem):
        self.eng, self.sem, self.n, self.base = eng, sem, 0, 0

    def done(self, ins):
        ins.then_inc(self.sem, 1)
        self.n += 1

    def settle(self):
        self.eng.wait_ge(self.sem, self.base + self.n)

    def enter(self, at, per_body):
        self.start, self.per_body = self.n, per_body
        self.base, self.n = self.start + at * per_body, 0

    def leave(self, times):
        assert self.n == self.per_body, (self.n, self.per_body)
        self.base, self.n = 0, self.start + times * self.per_body


def build(nc, x, ctx_in, wq, bq, wk, bk, wv, bv, gate_w, gate_b, w1, b1, w2, b2, cst, nyq, out, mem_scale):
    xn_dram = nc.dram_tensor("xn_rows", [TOK, D], F32, kind="Internal").ap()
    y_rows = CH * TOK + P * NCOL
    y_dram = nc.dram_tensor("y_rows", [y_rows, D], F32, kind="Internal").ap()
    tiles = lambda ap: ap.rearrange("(t p) d -> p t d", p=P)
    x_t, ctx_t, out_t, xn_t = tiles(x), tiles(ctx_in), tiles(out), tiles(xn_dram)

    with ExitStack() as ctx:
        def sb(name, shape, dt=F32):
            return ctx.enter_context(nc.sbuf_tensor(name, shape, dt))

        def sem(name):
            return ctx.enter_context(nc.semaphore(name))

        const = sb("const", [P, NCONST])
        shared_a = sb("shared_a", [P, NT * P])
        nyq_inv = shared_a[0:BATCH]
        xq = sb("xq", [P, CH, NT, D])
        x_sb, q_sb = xq[:, 0], xq[:, 1]
        ctx_sb = sb("ctx_sb", [P, NT, D])
        x1_sb = sb("x1_sb", [P, NT, D])
        w_raw = sb("w_raw", [P, 3, D])
        basis = sb("basis", [P, 3, 2, 2 * D])
        bias3 = sb("bias3", [3, 3, D])
        shared_b = sb("shared_b", [P, CH * NT * NCOL])
        bsplit = shared_b[0:3, 0:4 * 3 * D].rearrange("p (n d) -> p n d", n=4)
        bhalf = sb("bhalf", [3, 3, 3 * D], BF16)
        bbasis = sb("bbasis", [3, 3, 2 * D], BF16)
        dc3 = sb("dc3", [3, P], BF16)
        gw_sb = sb("gw_sb", [P, E])
        gb_sb = sb("gb_sb", [P, 1, E])
        w1_hi = sb("w1_hi", [P, E, 2 * FF], F32R)
        w1_lo = sb("w1_lo", [P, E, 2 * FF], F32R)
        w1_spare = sb("w1_spare", [P, 2, 2 * FF])
        w2_sb = sb("w2_sb", [P, E * FC, D])
        w1_raw = [x1_sb[:].rearrange("p (e t) d -> p e (t d)", e=2), w1_spare[:],
                  w2_sb[:].rearrange("p (e n) d -> p e (n d)", e=4)]
        b1_rows = sb("b1_rows", [E * 2 * FC, P])
        b2_sb = sb("b2_sb", [P, E, D])
        b1_col = sb("b1_col", [P, E * 2 * FC])
        stats = sb("stats", [P, NT, 6])
        tok = sb("tok", [P, 16, NT])
        spec = sb("spec", [P, 2, 2, 2, P])
        spec_n = sb("spec_n", [P, 2, BATCH])
        q_basis = sb("q_basis", [P, 2, 256])
        prod1 = sb("prod1", [P, 4, 256])
        half1 = sb("half1", [P, 4, 128])
        prod2 = sb("prod2", [P, 4, 256])
        half2 = sb("half2", [P, 4, 128])
        mat = sb("mat", [P, 2, 2, 64])
        mat2 = sb("mat2", [P, 2, 2, 64])
        sums = sb("sums", [P, 2, 14 * QUAD])
        q_n = sb("q_n", [BATCH, 256])
        prod_n = sb("prod_n", [BATCH, 4, 256])
        half_n = sb("half_n", [BATCH, 4, 128])
        mat_n = sb("mat_n", [BATCH, 2, 2, 64])
        mat2_n = sb("mat2_n", [BATCH, 2, 2, 64])
        sums_n = sb("sums_n", [BATCH, 14 * QUAD])
        logit = sb("logit", [P, NT, E])
        logit2 = sb("logit2", [P, NT, E])
        rt = sums[:].rearrange("p a b -> p (a b)")[:, 0:6 * NT * E].rearrange("p (n t e) -> p n t e", n=6, e=E)
        hot = sb("hot", [P, CH, NT, E])
        chosen = sb("chosen", [P, E, NT])
        ranks = sb("ranks", [P, E, NT])
        slot_e = sb("slot_e", [P, E, NT])
        ex = sb("ex", [P, 10, E])
        ex2 = sb("ex2", [P, E, E])
        rowsum = sb("rowsum", [P, E], BF16)
        tri_b = sb("tri_b", [P, P], BF16)
        ones_b = sb("ones_b", [P, P], BF16)
        bounds = sb("bounds", [P, E], I32)
        slot = sb("slot", [P, CH * NT])
        slot_i = sb("slot_i", [P, 3, CH * NT], I32)
        slot_f = sb("slot_f", [P, 2, CH * NT], BF16)
        iota_b = sb("iota_b", [P, P], BF16)
        choice_b = sb("choice_b", [P, CH * NT], BF16)
        hot_lo = shared_a[:].bitcast(BF16).rearrange("p (n q) -> p n q", q=P)
        hot_hi = basis[:].rearrange("p s m d -> p (s m d)")[:, 0:CH * NT * NCOL // 2].bitcast(BF16).rearrange(
            "p (n c) -> p n c", c=NCOL)
        hot_val = shared_b[:].bitcast(BF16).rearrange("p (n a c) -> p n a c", a=2, c=NCOL)
        row = sb("row", [P, 6, NCOL])
        lists_all = sb("lists_all", [P, MAX_TILES + 2 * AHEAD, 2, HALVES], I32)
        taken, taken_a = sb("taken", [1, 2]), sb("taken_a", [1, 1])
        lists_now = sb("lists_now", [P, 2, 2, HALVES], I32)
        xg, y_sb = spec[:, 0], spec[:, 1]
        xT_hi = sb("xT_hi", [P, XT], F32R)
        xT_lo = sb("xT_lo", [P, XT], F32R)
        act, silu = prod1, prod2
        x_now = sb("x_now", [P, HALVES, D])
        y_in = xq
        xnT = res = ctx_sb

        bank = ctx.enter_context(nc.psum_tensor("bank", [P, 8, 512], F32))

        def C(name, rows=P):
            return const[0:rows, COL[name][0]:COL[name][1]]

        def sums_from(m2, s):
            n0 = m2[:, 0].rearrange("p q (c d) -> p q c d", d=QUAD)
            n1 = m2[:, 1].rearrange("p q (c d) -> p q c d", d=QUAD)
            add = s.rearrange("p (q r d) -> p q r d", q=2, d=QUAD)[:, :, 0:5:4]
            sub = s[:, 3 * QUAD:9 * QUAD].rearrange("p (q r d) -> p q r d", q=2, d=QUAD)[:, :, 0:3:2]
            return (add, n0[:, :, ::-1], n1), (sub, n0[:, ::-1, ::-1], n1[:, ::-1])

        const_in, rest_in, ctx_in_s, w_in, small_in = (sem(n) for n in ("const_in", "rest_in", "ctx_in", "w_in", "small_in"))
        x_in = [sem(f"x_in{c}") for c in range(2)]
        bias_in, b1_in, w1_hi_ready, w1_ready = (sem(n) for n in ("bias_in", "b1_in", "w1_hi_ready", "w1_ready"))
        w1_in = [sem(f"w1_in{i}") for i in range(3)]
        w2_in, nyq_in = sem("w2_in"), sem("nyq_in")
        w_turned, basis_ready, parts_ready, bias_ready, b1_turned, b1_ready = (
            sem(n) for n in ("w_turned", "basis_ready", "parts_ready", "bias_ready", "b1_turned", "b1_ready"))
        v_step, p_step, a_step = sem("v_step"), sem("p_step"), sem("a_step")
        var_ready, sd_ready, norm_ready, exp_ready, scale_ready = (
            sem(n) for n in ("var_ready", "sd_ready", "norm_ready", "exp_ready", "scale_ready"))
        q_ready, nyq_dft, nyq_spec, nyq_proj, nyq_q, nyq_prod, nyq_half, nyq_sums = (
            sem(n) for n in ("q_ready", "nyq_dft", "nyq_spec", "nyq_proj", "nyq_q", "nyq_prod", "nyq_half", "nyq_sums"))
        q_basis_ready = sem("q_basis_ready")
        dft_done, spec_ready, proj_done, prod1_ready, half1_ready, prod2_ready, half2_ready, sums_ready, att_done, x1_ready = (
            sem(n) for n in ("dft_done", "spec_ready", "proj_done", "prod1_ready", "half1_ready", "prod2_ready",
                             "half2_ready", "sums_ready", "att_done", "x1_ready"))
        var2_ready, sd2_ready, scale2_ready, xn_ready, xn_out, xn_turned, xnT_first, xnT_ready, gate_done = (
            sem(n) for n in ("var2_ready", "sd2_ready", "scale2_ready", "xn_ready", "xn_out", "xn_turned",
                             "xnT_first", "xnT_ready", "gate_done"))
        gap_ready, gap_exp, rowsum_ready, counted, bounds_ready, hot_hi_ready, hot_p_ready, hot_c_ready, hots_ready, listed, rows_ready = (
            sem(n) for n in ("gap_ready", "gap_exp", "rowsum_ready", "counted", "bounds_ready", "hot_hi_ready", "hot_p_ready", "hot_c_ready", "hots_ready",
                             "listed", "rows_ready"))
        gathered = [[sem(f"gathered{par}{h}") for h in range(HALVES)] for par in range(2)]
        scattered = [[sem(f"scattered{par}{h}") for h in range(HALVES)] for par in range(2)]
        x_moved, xT_turned, xT_hi_ready, xT_ready, up_done, silu_ready, act_ready, down_done, y_ready = (
            sem(n) for n in ("x_moved", "xT_turned", "xT_hi_ready", "xT_ready", "up_done", "silu_ready", "act_ready", "down_done", "y_ready"))
        lists_taken = sem("lists_taken")
        y_in_s = [sem(f"y_in{c}") for c in range(4)]
        p_ready, second_ready, res_ready, out_done = (sem(n) for n in ("p_ready", "second_ready", "res_ready", "out_done"))

        block = ctx.enter_context(nc.Block())

        @block.sync
        def _(sp):
            for c in range(2):
                sp.dma_start(x_sb[:, 8 * c:8 * c + 8, :], x_t[:, 8 * c:8 * c + 8, :]).then_inc(x_in[c], 16)
            sp.dma_start(ctx_sb[:], ctx_t).then_inc(ctx_in_s, 16)
            sp.dma_start(const[:, NFIRST:], cst[:, NFIRST:]).then_inc(rest_in, 16)
            sp.dma_start(nyq_inv[:], nyq).then_inc(nyq_in, 16)
            sp.wait_ge(small_in, 48)
            for i, (first, end) in enumerate(((0, 2), (2, 4), (4, E))):
                sp.dma_start(w1_raw[i], w1[first:end].rearrange("e d h -> d e h")).then_inc(w1_in[i], 16)
            for c in range(4):
                sp.wait_ge(xn_ready, 4 * (c + 1))
                sp.dma_start(xn_t[:, 4 * c:4 * c + 4, :], q_sb[:, 4 * c:4 * c + 4, :]).then_inc(xn_out, 16)
            sp.wait_ge(w1_ready, E)
            sp.dma_start(w2_sb[:], w2.rearrange("e (c f) d -> f (e c) d", f=P)).then_inc(w2_in, 16)
            sp.wait_ge(bounds_ready, 1)
            last = sp.value_load(bounds[0:1, E - 1:E], min_val=E, max_val=MAX_TILES)
            for h in range(HALVES):
                sp.wait_ge(scattered[0][h], ((last + 1) // 2) * 16 + 16)
                sp.wait_ge(scattered[1][h], (last // 2) * 16 + 32)
            sp.wait_ge(xn_out, 64)
            y_back = y_dram[0:CH * TOK].rearrange("(c t p) d -> p c t d", p=P, c=CH)
            for c in range(4):
                for j in range(CH):
                    sp.dma_start(y_in[:, j, 4 * c:4 * c + 4, :], y_back[:, j, 4 * c:4 * c + 4, :]).then_inc(y_in_s[c], 16)
            for c in range(4):
                sp.wait_ge(res_ready, c + 1)
                sp.dma_start(out_t[:, 4 * c:4 * c + 4, :], res[:, 4 * c:4 * c + 4, :]).then_inc(out_done, 16)
            sp.wait_ge(out_done, 64)

        @block.scalar
        def _(a):
            a.dma_start(const[:, 0:NFIRST], cst[:, 0:NFIRST]).then_inc(const_in, 16)
            for i, b in enumerate((bq, bk, bv)):
                a.dma_start(bias3[:, i, :], b.partition_broadcast(3)).then_inc(bias_in, 16)
            for i, w in enumerate((wq, wk, wv)):
                a.dma_start(w_raw[:, i, :], w).then_inc(w_in, 16)
            a.dma_start(b1_rows[:], b1.rearrange("e (c f) -> (e c) f", f=P)).then_inc(b1_in, 16)
            a.dma_start(b2_sb[:].rearrange("p e d -> p (e d)"),
                        b2.rearrange("e d -> (e d)").partition_broadcast(P)).then_inc(small_in, 16)
            a.dma_start(gw_sb[:], gate_w).then_inc(small_in, 16)
            a.dma_start(gb_sb[:, 0, :], gate_b.partition_broadcast(P)).then_inc(small_in, 16)
            a.wait_ge(var_ready, 1)
            nc.scalar.activation(tok[:, 3, :], tok[:, 2, :], ACT.Sqrt).then_inc(sd_ready, 1)
            nc.scalar.activation(tok[:, 6, :], tok[:, 1, :], ACT.Sqrt, scale=float(D)).then_inc(sd_ready, 1)
            nc.scalar.activation(taken_a[:], tok[0:1, 2, 0:1], ACT.Exp)
            a.wait_ge(norm_ready, 1)
            nc.scalar.activation(tok[:, 7, :], tok[:, 5, :], ACT.Exp, scale=-1.0).then_inc(exp_ready, 1)
            a.wait_ge(w_turned, 1)
            turned = bank[:, 6, 0:3 * D].rearrange("p (s d) -> p s d", s=3)

            def to_basis(m, table):
                for (r, ri, c), (part, sign) in table.items():
                    at = r * 128 + ri * 64 + c * QUAD
                    nc.scalar.activation(basis[:, :, m, at:at + QUAD], turned[:, :, part * QUAD:(part + 1) * QUAD],
                                         ACT.Copy, scale=float(sign)).then_inc(basis_ready, 1)

            to_basis(0, FROM_RE)
            to_basis(1, FROM_IM)
            def high_parts(i):
                a.wait_ge(w1_in[i], 16)
                for j in range(2):
                    nc.scalar.activation(w1_hi[:, 2 * i + j, :], w1_raw[i][:, j, :], ACT.Copy).then_inc(w1_hi_ready, 1)

            high_parts(0)
            a.wait_ge(scale_ready, 1)
            def normalise(tiles):
                for t in tiles:
                    nc.scalar.activation(q_sb[:, t, :], x_sb[:, t, :], ACT.Identity,
                                         bias=tok[:, 10, t:t + 1], scale=tok[:, 9, t:t + 1]).then_inc(q_ready, 1)

            def keep_spectra(g, par):
                a.wait_ge(dft_done, g + 1)
                nc.scalar.activation(spec[:, par].rearrange("p s r n -> p (s r n)"), bank[:, par, :],
                                     ACT.Copy).then_inc(spec_ready, 1)

            def keep_q(g, par):
                a.wait_ge(proj_done, g + 1)
                nc.scalar.activation(q_basis[:, par, :], bank[:, 2 + par, 0:256], ACT.Copy).then_inc(q_basis_ready, 1)

            normalise(range(0, 4))
            keep_spectra(0, 0)
            normalise(range(4, 8))
            keep_spectra(1, 1)
            keep_q(0, 0)
            normalise(range(8, 12))
            keep_q(1, 1)
            normalise(range(12, NT))
            keep_spectra(2, 0)
            a.wait_ge(nyq_dft, 1)
            nc.scalar.activation(spec_n[:], bank[:, 7, 0:2 * BATCH], ACT.Copy).then_inc(nyq_spec, 1)
            a.wait_ge(nyq_proj, 1)
            nc.scalar.activation(q_n[:], bank[0:BATCH, 6, 0:256], ACT.Copy).then_inc(nyq_q, 1)
            high_parts(1)
            a.wait_ge(w1_in[2], 16)
            with a.Fori(1, G // 2 - 1) as i:
                for par in range(2):
                    keep_q(2 * i + par, par)
                    keep_spectra(2 * i + par + 1, 1 - par)
                    nc.scalar.activation(w1_hi[:, bass.ds(2 * i + par + 2, 1), :], w1_raw[2][:, bass.ds(2 * i + par - 2, 1), :],
                                         ACT.Copy).then_inc(w1_hi_ready, 1)
            keep_q(G - 2, 0)
            keep_spectra(G - 1, 1)
            keep_q(G - 1, 1)
            def keep_xnT(b):
                a.wait_ge(xn_turned, b + 1)
                nc.scalar.activation(xnT[:, 4 * b:4 * b + 4, :].rearrange("p t n -> p (t n)"), bank[:, b, :],
                                     ACT.Copy).then_inc(xnT_first, 1)

            for n, part in enumerate((range(0, NT - 4), range(NT - 4, NT))):
                at = slice(part[0], part[-1] + 1)
                a.wait_ge(var2_ready, n + 1)
                nc.scalar.activation(tok[:, 3, at], tok[:, 2, at], ACT.Sqrt).then_inc(sd2_ready, 1)
                if n == 1:
                    keep_xnT(1)
                a.wait_ge(scale2_ready, n + 1)
                for t in part:
                    if t == 9:
                        keep_xnT(0)
                    nc.scalar.activation(q_sb[:, t, :], x1_sb[:, t, :], ACT.Identity,
                                         bias=tok[:, 10, t:t + 1], scale=tok[:, 4, t:t + 1]).then_inc(xn_ready, 1)
            a.wait_ge(gap_ready, 1)
            nc.scalar.activation(tok[:, 13, :], tok[:, 12, :], ACT.Exp).then_inc(gap_exp, 1)
            for j in range(CH):
                n = slice(j * NT, (j + 1) * NT)
                a.wait_ge(hot_hi_ready, j + 1)
                nc.scalar.activation(hot_val[:, n, 0, :], hot_hi[:, n], ACT.Copy, scale=C("pcol")).then_inc(hot_p_ready, 1)
            nc.scalar.activation(taken_a[:], C("pcol", 1), ACT.Silu)
            def keep_xT_hi(n):
                a.wait_ge(xT_turned, n + 1)
                nc.scalar.activation(xT_hi[:], bank[:, 4, 0:XT], ACT.Copy).then_inc(xT_hi_ready, 1)

            a.wait_ge(bounds_ready, 1)
            ends = [a.value_load(bounds[0:1, e:e + 1], min_val=e + 1, max_val=MAX_TILES) for e in range(E)]
            keep_xT_hi(0)
            a.wait_ge(b1_ready, 1)
            for e in range(E):
                with a.Fori(ends[e - 1] if e else 0, ends[e]) as t:
                    for c in range(FC):
                        a.wait_ge(up_done, FC * t + c + 1)
                        nc.scalar.activation(silu[:, c, :], bank[:, c, XT:2 * XT], ACT.Silu,
                                             bias=b1_col[:, e * 2 * FC + FC + c:e * 2 * FC + FC + c + 1]).then_inc(silu_ready, 1)
                    keep_xT_hi(t + 1)
            a.wait_ge(p_ready, 1)
            for c in range(4):
                a.wait_ge(y_in_s[c], 32)
                for t in range(4 * c, 4 * c + 4):
                    nc.scalar.activation(y_in[:, 1, t, :], y_in[:, 1, t, :], ACT.Copy,
                                         scale=tok[:, 7, t:t + 1]).then_inc(second_ready, 1)

        @block.vector
        def _(v):
            st = Steps(v, v_step)

            def op(fn, *args, **kw):
                if st.n:
                    st.settle()
                st.done(fn(*args, **kw))

            tt, ts, stt, cp = nc.vector.tensor_tensor, nc.vector.tensor_scalar, nc.vector.scalar_tensor_tensor, nc.vector.tensor_copy

            def ln_moments(part):
                me, mo, ve, vo = (stats[:, part, j] for j in (1, 4, 2, 5))
                st.done(tt(tok[:, 0, part], me, mo, ALU.add))
                st.done(tt(tok[:, 1, part], me, mo, ALU.subtract))
                st.done(tt(tok[:, 2, part], ve, vo, ALU.add))
                st.settle()
                st.done(ts(tok[:, 0, part], tok[:, 0, part], 0.5, None, ALU.mult))
                st.done(tt(tok[:, 1, part], tok[:, 1, part], tok[:, 1, part], ALU.mult))
                op(stt, tok[:, 1, part], tok[:, 1, part], D / 4.0, tok[:, 2, part], ALU.mult, ALU.add)
                st.settle()
                st.done(ts(tok[:, 2, part], tok[:, 1, part], 1.0 / D, LN_EPS, ALU.mult, ALU.add))
                return ts(tok[:, 1, part], tok[:, 1, part], 1.0 / D, None, ALU.mult)

            def ln_rstd(part):
                st.done(nc.vector.reciprocal(tok[:, 4, part], tok[:, 3, part]))
                op(tt, tok[:, 5, part], tok[:, 4, part], tok[:, 4, part], ALU.mult)
                op(tt, tok[:, 5, part], tok[:, 5, part], tok[:, 2, part], ALU.mult)
                op(ts, tok[:, 5, part], tok[:, 5, part], -0.5, 1.5, ALU.mult, ALU.add)
                op(tt, tok[:, 4, part], tok[:, 4, part], tok[:, 5, part], ALU.mult)

            every = slice(0, NT)
            for c in range(2):
                v.wait_ge(x_in[c], 16)
                for t in range(8 * c, 8 * c + 8):
                    st.done(nc.vector.bn_stats(stats[:, t, :], x_sb[:, t, :]))
            st.settle()
            ln_moments(every).then_inc(var_ready, 1)
            v.wait_ge(var_ready, 1)
            v.wait_ge(sd_ready, 2)
            ln_rstd(every)
            st.settle()
            tt(tok[:, 5, :], tok[:, 4, :], tok[:, 6, :], ALU.mult).then_inc(norm_ready, 1)
            v.wait_ge(exp_ready, 1)
            op(ts, tok[:, 8, :], tok[:, 7, :], 1.0, None, ALU.add)
            op(nc.vector.reciprocal, tok[:, 8, :], tok[:, 8, :])
            for _ in range(LOGISTIC_N):
                op(ts, tok[:, 7, :], tok[:, 8, :], -1.0, 1.0, ALU.mult, ALU.add)
                op(stt, tok[:, 8, :], tok[:, 8, :], LOGISTIC_R, tok[:, 7, :], ALU.mult, ALU.mult)
            op(ts, tok[:, 8, :], tok[:, 8, :], 0.1, 0.95, ALU.mult, ALU.add)
            v.wait_ge(const_in, 16)
            op(stt, tok[:, 9, :], tok[:, 8, :], C("wave"), tok[:, 4, :], ALU.mult, ALU.mult)
            st.settle()
            stt(tok[:, 10, :], tok[:, 9, :], -1.0, tok[:, 0, :], ALU.mult, ALU.mult).then_inc(scale_ready, 1)
            st.done(cp(dc3[:], C("dc", 3)))
            v.wait_ge(parts_ready, 1)
            parts = bsplit[:, 2, :].rearrange("p (s d) -> p s d", s=3)
            for (r, ri, c), (part, sign) in FROM_RE.items():
                at = r * 128 + ri * 64 + c * QUAD
                ts(bbasis[:, :, at:at + QUAD], parts[:, :, part * QUAD:(part + 1) * QUAD], float(sign), None,
                   ALU.mult).then_inc(bias_ready, 1)
            v.wait_ge(b1_turned, 1)
            cp(b1_col[:], bank[:, 5, 0:E * 2 * FC]).then_inc(b1_ready, 1)
            v.wait_ge(rest_in, 16)
            st.done(cp(tri_b[:], C("tri")))
            st.done(cp(ones_b[:], C("ones")))
            st.done(cp(iota_b[:], C("iota")))
            st.done(cp(choice_b[:], C("choice")))

            def multiply(left, right_of, prod, rows=P):
                for i in range(2):
                    for qri in range(2):
                        l = left(i, qri).unsqueeze(2).to_broadcast([rows, 2, 4, QUAD])
                        r = right_of.rearrange("p (j m c) -> p j m c", j=2, c=QUAD)
                        o = prod[:, 2 * i + qri, :].rearrange("p (j m c) -> p j m c", j=2, c=QUAD)
                        last = tt(o, l, r, ALU.mult)
                return last

            def combine(half, dst):
                h = half[:].rearrange("p (i q) n -> p i q n", i=2)
                st.done(tt(dst[:, :, 0, :], h[:, :, 0, 0:64], h[:, :, 1, 64:128], ALU.subtract))
                st.done(tt(dst[:, :, 1, :], h[:, :, 0, 64:128], h[:, :, 1, 0:64], ALU.add))

            def residual(g, par):
                v.wait_ge(att_done, g + 1)
                pair = bass.ds(2 * g, 2)
                tt(x1_sb[:, pair, :], x_sb[:, pair, :], bank[:, 6 + par, 0:256].rearrange("p (t d) -> p t d", t=2),
                   ALU.add).then_inc(x1_ready, 1)

            def residual_stats(g):
                v.wait_ge(x1_ready, g + 1)
                for j in range(2):
                    st.done(nc.vector.bn_stats(stats[:, bass.ds(2 * g + j, 1), :], x1_sb[:, bass.ds(2 * g + j, 1), :]))

            def finish(g, par):
                v.wait_ge(half2_ready, g + 1)
                combine(half2, mat2)

            def finish_sums(g, par):
                (o, n0, n1), (o2, m0, m1) = sums_from(mat2, sums[:, par])
                tt(o, n0, n1, ALU.add)
                tt(o2, m0, m1, ALU.subtract).then_inc(sums_ready, 1)

            def stage(g, par, residuals, has_before=True, beside=None):
                qk = bank[:, 2 + par, :].rearrange("p (s n) -> p s n", s=2)
                left = lambda i, q: q_basis[:, par, :].rearrange(
                    "p (i q j c) -> p i q j c", i=2, q=2, c=QUAD)[:, i, q]
                v.wait_ge(q_basis_ready, g + 1)
                multiply(left, qk[:, 1, :], prod1).then_inc(prod1_ready, 1)
                if has_before:
                    finish(g - 1, 1 - par)
                for r, p in residuals:
                    residual(r, p)
                if has_before:
                    st.settle()
                    finish_sums(g - 1, 1 - par)
                if beside:
                    beside()
                v.wait_ge(half1_ready, g + 1)
                combine(half1, mat)
                for r, p in residuals:
                    residual_stats(r)
                st.settle()
                m = lambda i, q: mat[:, i, q, :].rearrange("p (j c) -> p j c", c=QUAD)
                multiply(m, bank[:, 4 + par, 0:256], prod2).then_inc(prod2_ready, 1)

            STAGE_STEPS = 2 + 2 + 2

            stage(0, 0, [], has_before=False)
            stage(1, 1, [])
            by_row = lambda ap: ap.rearrange("p (i q j c) -> p i q j c", i=2, q=2, c=QUAD)
            v.wait_ge(nyq_q, 1)
            multiply(lambda i, q: by_row(q_n[:])[:, i, q], bank[0:BATCH, 6, 256:512], prod_n, BATCH).then_inc(nyq_prod, 1)

            def nyquist_v():
                v.wait_ge(nyq_half, 1)
                combine(half_n, mat_n)
                st.settle()
                multiply(lambda i, q: mat_n[:, i, q, :].rearrange("p (j c) -> p j c", c=QUAD),
                         bank[0:BATCH, 7, 128:384], prod_n, BATCH).then_inc(nyq_prod, 1)

            stage(2, 0, [], beside=nyquist_v)
            v.wait_ge(nyq_half, 2)
            combine(half_n, mat2_n)
            st.settle()
            (o, n0, n1), (o2, m0, m1) = sums_from(mat2_n, sums_n)
            tt(o, n0, n1, ALU.add)
            tt(o2, m0, m1, ALU.subtract).then_inc(nyq_sums, 1)
            v.wait_ge(w1_ready, 2)
            stage(3, 1, [(0, 0), (1, 1)])
            with v.Fori(2, G // 2) as i:
                st.enter(i - 2, 2 * STAGE_STEPS)
                for par in range(2):
                    g = 2 * i + par
                    stage(g, par, [(g - 2, par)])
                st.leave(G // 2 - 2)
            first = slice(0, NT - 4)
            rest = slice(NT - 4, NT)
            st.settle()
            ln_moments(first).then_inc(var2_ready, 1)
            finish(G - 1, 1)
            st.settle()
            finish_sums(G - 1, 1)

            def scale2(part, n):
                v.wait_ge(var2_ready, n)
                v.wait_ge(sd2_ready, n)
                ln_rstd(part)
                st.settle()
                stt(tok[:, 10, part], tok[:, 4, part], -1.0, tok[:, 0, part], ALU.mult, ALU.mult).then_inc(scale2_ready, 1)

            scale2(first, 1)
            residual(G - 2, 0)
            residual_stats(G - 2)
            residual(G - 1, 1)
            residual_stats(G - 1)
            st.settle()
            ln_moments(rest).then_inc(var2_ready, 1)
            scale2(rest, 2)

            def keep_xnT(b):
                v.wait_ge(xn_turned, b + 1)
                cp(xnT[:, 4 * b:4 * b + 4, :].rearrange("p t n -> p (t n)"), bank[:, b, :]).then_inc(xnT_ready, 1)

            keep_xnT(2)

            HALF = NT // 2
            wide = lambda ap: ap.unsqueeze(2).to_broadcast([P, HALF, E])
            rev = C("rev").unsqueeze(1).to_broadcast([P, HALF, E])
            v.wait_ge(small_in, 48)

            def choose(part, src, best, onehot):
                op(nc.vector.tensor_reduce, best, src, AX, ALU.max)
                op(tt, rt[:, 0, part], src, wide(best), ALU.is_equal)
                op(tt, rt[:, 1, part], rt[:, 0, part], rev, ALU.mult)
                op(nc.vector.tensor_reduce, tok[:, 14, part], rt[:, 1, part], AX, ALU.max)
                op(tt, onehot, rev, wide(tok[:, 14, part]), ALU.is_equal)

            for n, part in enumerate((slice(0, HALF), slice(HALF, NT))):
                v.wait_ge(gate_done, part.stop)
                op(tt, logit[:, part], bank[:, 4 + n, part.start * E:part.stop * E].rearrange("p (t e) -> p t e", e=E),
                   gb_sb[:].to_broadcast([P, HALF, E]), ALU.add)
                choose(part, logit[:, part], tok[:, 11, part], hot[:, 0, part])
                op(stt, logit2[:, part], hot[:, 0, part], NEG, logit[:, part], ALU.mult, ALU.add)
                if n == 0:
                    keep_xnT(3)
                choose(part, logit2[:, part], tok[:, 15, part], hot[:, 1, part])
            st.settle()
            by_e = lambda ap: ap.rearrange("p t e -> p e t")
            st.done(tt(chosen[:], by_e(hot[:, 0]), by_e(hot[:, 1]), ALU.add))
            tt(tok[:, 12, :], tok[:, 15, :], tok[:, 11, :], ALU.subtract).then_inc(gap_ready, 1)
            op(nc.vector.tensor_tensor_scan, ranks[:].rearrange("p e t -> p (e t)"), C("reset"),
               chosen[:].rearrange("p e t -> p (e t)"), 0.0, ALU.mult, ALU.add)
            st.settle()
            cp(rowsum[:], ranks[:, :, NT - 1]).then_inc(rowsum_ready, 1)
            v.wait_ge(counted, 1)
            op(cp, ex[:, 0, :], bank[:, 3, E:2 * E])
            op(tt, ex2[:], ex[:, 0, :].unsqueeze(2).to_broadcast([P, E, E]),
               C("steps").unsqueeze(1).to_broadcast([P, E, E]), ALU.is_gt)
            op(nc.vector.tensor_reduce, ex[:, 1, :], ex2[:], AX, ALU.add)
            op(ts, ex[:, 1, :], ex[:, 1, :], 1.0, None, ALU.max)
            op(nc.vector.tensor_tensor_scan, ex[:, 2, :], C("ones")[:, 0:E], ex[:, 1, :], 0.0, ALU.mult, ALU.add)
            op(tt, ex[:, 3, :], ex[:, 2, :], ex[:, 1, :], ALU.subtract)
            cp(bounds[:], ex[:, 2, :]).then_inc(bounds_ready, 1)
            op(stt, ex[:, 4, :], ex[:, 3, :], float(XT), bank[:, 3, 0:E], ALU.mult, ALU.add)
            op(tt, slot_e[:], ranks[:], chosen[:], ALU.subtract)
            op(tt, slot_e[:], slot_e[:], ex[:, 4, :].unsqueeze(2).to_broadcast([P, E, NT]), ALU.add)
            st.settle()
            for j in range(CH):
                st.done(tt(rt[:, 2 + j], hot[:, j], slot_e[:].rearrange("p e t -> p t e"), ALU.mult))
            st.settle()
            for j in range(CH):
                st.done(nc.vector.tensor_reduce(slot[:, j * NT:(j + 1) * NT], rt[:, 2 + j], AX, ALU.add))
            op(cp, slot_i[:, 0, :], slot[:])
            st.settle()
            st.done(ts(slot_i[:, 1, :], slot_i[:, 0, :], 7, None, ALU.logical_shift_right))
            st.done(ts(slot_i[:, 2, :], slot_i[:, 0, :], P - 1, None, ALU.bitwise_and))
            op(cp, slot_f[:], slot_i[:, 1:3, :])
            st.settle()
            for j in range(CH):
                n = slice(j * NT, (j + 1) * NT)
                shape_hi = [P, NT, NCOL]
                tt(hot_hi[:, n], iota_b[:, 0:NCOL].unsqueeze(1).to_broadcast(shape_hi),
                   slot_f[:, 0, n].unsqueeze(2).to_broadcast(shape_hi), ALU.is_equal).then_inc(hot_hi_ready, 1)
            for first, end in HOT_PARTS:
                n = slice(first, end)
                shape_lo = [P, end - first, P]
                tt(hot_lo[:, n], iota_b[:].unsqueeze(1).to_broadcast(shape_lo),
                   slot_f[:, 1, n].unsqueeze(2).to_broadcast(shape_lo), ALU.is_equal).then_inc(hots_ready, 1)
            by_tile = lambda ap: ap.rearrange("p (t h) -> p t h", h=HALVES)
            v.wait_ge(listed, 1)
            op(cp, row[:, 5, :], bank[:, 7, 0:NCOL])
            op(stt, row[:, 0, :], bank[:, 7, NCOL:2 * NCOL], float(P), row[:, 5, :], ALU.mult, ALU.add)
            op(ts, row[:, 3, :], row[:, 0, :], float(P + TOK), float(-TOK), ALU.is_ge, ALU.mult)
            st.done(ts(row[:, 1, :], row[:, 0, :], 0.0, None, ALU.is_equal))
            op(stt, row[:, 4, :], row[:, 0, :], float(-P), row[:, 3, :], ALU.add, ALU.add)
            st.done(tt(row[:, 2, :], row[:, 1, :], C("dummy"), ALU.mult))
            st.settle()
            ts(lists_all[:, 0:MAX_TILES + AHEAD, 0, :], by_tile(row[:, 4, :]), 0.0, None, ALU.max).then_inc(rows_ready, 1)
            op(tt, row[:, 2, :], row[:, 2, :], row[:, 0, :], ALU.add)
            st.settle()
            ts(lists_all[:, AHEAD:, 1, :], by_tile(row[:, 2, :]), float(-P), None, ALU.add).then_inc(rows_ready, 1)
            v.wait_ge(gap_exp, 1)
            op(ts, tok[:, 5, :], tok[:, 13, :], 1.0, None, ALU.add)
            op(nc.vector.reciprocal, tok[:, 6, :], tok[:, 5, :])
            st.settle()
            tt(tok[:, 7, :], tok[:, 13, :], tok[:, 6, :], ALU.mult).then_inc(p_ready, 1)

            def keep_xT(n):
                v.wait_ge(xT_hi_ready, n + 1)
                tt(xT_lo[:], bank[:, 4, 0:XT], xT_hi[:].bitcast(F32), ALU.subtract).then_inc(xT_ready, 1)

            def move_x(n):
                cp(x_now[:], xg[:, bass.ds(n % 2, 1)].rearrange("p o h d -> p (o h) d")).then_inc(x_moved, 1)

            v.wait_ge(bounds_ready, 1)
            ends = [v.value_load(bounds[0:1, e:e + 1], min_val=e + 1, max_val=MAX_TILES) for e in range(E - 3)]
            for h in range(HALVES):
                v.wait_ge(gathered[0][h], 16)
            move_x(0)
            keep_xT(0)
            for h in range(HALVES):
                v.wait_ge(gathered[1][h], 16)
            move_x(1)
            ends += [v.value_load(bounds[0:1, e:e + 1], min_val=e + 1, max_val=MAX_TILES) for e in range(E - 3, E)]
            for e in range(E):
                with v.Fori(ends[e - 1] if e else 0, ends[e]) as t:
                    v.wait_ge(down_done, t + 1)
                    for c in range(FC):
                        v.wait_ge(silu_ready, FC * t + c + 1)
                        stt(act[:, c, :], bank[:, c, 0:XT], b1_col[:, e * 2 * FC + c:e * 2 * FC + c + 1],
                            silu[:, c, :], ALU.add, ALU.mult).then_inc(act_ready, 1)
                    keep_xT(t + 1)
                    v.wait_ge(down_done, t + 2)
                    for h in range(HALVES):
                        v.wait_ge(scattered[0][h], (t // 2) * 16 + 16)
                        v.wait_ge(scattered[1][h], ((t + 1) // 2) * 16 + 16)
                    tt(y_sb[:, bass.ds(t % 2, 1)].rearrange("p o h d -> p (o h) d"), bank[:, 5:7, 0:D],
                       b2_sb[:, e:e + 1, :].to_broadcast([P, HALVES, D]), ALU.add).then_inc(y_ready, 1)
                    for h in range(HALVES):
                        v.wait_ge(gathered[0][h], (t // 2) * 16 + 32)
                        v.wait_ge(gathered[1][h], ((t + 1) // 2) * 16 + 16)
                    move_x(t + 2)

            st.settle()
            for c in range(4):
                v.wait_ge(y_in_s[c], 32)
                four = slice(4 * c, 4 * c + 4)
                for t in range(4 * c, 4 * c + 4):
                    st.done(stt(res[:, t, :], y_in[:, 0, t, :], tok[:, 6, t:t + 1], x1_sb[:, t, :], ALU.mult, ALU.add))
                st.settle()
                v.wait_ge(second_ready, 4 * c + 4)
                tt(res[:, four, :], res[:, four, :], y_in[:, 1, four, :], ALU.add).then_inc(res_ready, 1)

        @block.gpsimd
        def _(p):
            st = Steps(p, p_step)
            tt = nc.gpsimd.tensor_tensor

            p.wait_ge(bias_in, 48)
            p.wait_ge(const_in, 16)
            flat = bias3[:, :, :].rearrange("p s d -> p (s d)")
            copy = nc.gpsimd.tensor_copy
            pick = lambda i: C("pick", 3)[:, i:i + 1].to_broadcast([3, 3 * D])

            def chain(fn, *args):
                if st.n:
                    st.settle()
                st.done(fn(*args))

            chain(copy, bhalf[:, 0, :], flat)
            chain(tt, bsplit[:, 0, :], flat, bhalf[:, 0, :], ALU.subtract)
            chain(copy, bhalf[:, 1, :], bsplit[:, 0, :])
            chain(tt, bsplit[:, 1, :], bsplit[:, 0, :], bhalf[:, 1, :], ALU.subtract)
            chain(tt, bsplit[:, 0, :], bhalf[:, 0, :], pick(0), ALU.mult)
            chain(tt, bsplit[:, 2, :], bhalf[:, 1, :], pick(1), ALU.mult)
            chain(tt, bsplit[:, 3, :], bsplit[:, 1, :], pick(2), ALU.mult)
            chain(tt, bsplit[:, 0, :], bsplit[:, 0, :], bsplit[:, 2, :], ALU.add)
            st.settle()
            tt(bsplit[:, 2, :], bsplit[:, 0, :], bsplit[:, 3, :], ALU.add).then_inc(parts_ready, 1)

            def low_parts(experts):
                for e in experts:
                    i = min(e // 2, 2)
                    p.wait_ge(w1_in[i], 16)
                    p.wait_ge(w1_hi_ready, e + 1)
                    tt(w1_lo[:, e, :], w1_raw[i][:, e - 2 * i, :], w1_hi[:, e, :].bitcast(F32), ALU.subtract).then_inc(w1_ready, 1)

            low_parts(range(2))

            def add_halves(g):
                p.wait_ge(prod1_ready, g + 1)
                tt(half1[:], prod1[:, :, 0:128], prod1[:, :, 128:256], ALU.add).then_inc(half1_ready, 1)
                p.wait_ge(prod2_ready, g + 1)
                tt(half2[:], prod2[:, :, 0:128], prod2[:, :, 128:256], ALU.add).then_inc(half2_ready, 1)

            add_halves(0)
            add_halves(1)
            p.wait_ge(nyq_prod, 1)
            tt(half_n[:], prod_n[:, :, 0:128], prod_n[:, :, 128:256], ALU.add).then_inc(nyq_half, 1)
            p.wait_ge(prod1_ready, 3)
            tt(half1[:], prod1[:, :, 0:128], prod1[:, :, 128:256], ALU.add).then_inc(half1_ready, 1)
            p.wait_ge(nyq_prod, 2)
            tt(half_n[:], prod_n[:, :, 0:128], prod_n[:, :, 128:256], ALU.add).then_inc(nyq_half, 1)
            p.wait_ge(prod2_ready, 3)
            tt(half2[:], prod2[:, :, 0:128], prod2[:, :, 128:256], ALU.add).then_inc(half2_ready, 1)
            with p.Fori(3, G) as g:
                add_halves(g)

            low_parts(range(2, E))

            for n, (par, h) in enumerate((par, h) for par, h in ((0, 0), (0, 1), (1, 0), (1, 1), (1, 0), (1, 1))):
                at = CH * TOK + P * HALVES * MAX_TILES + 32 * n
                p.dma_start(y_dram[at:at + 32], const[0:32, 0:D]).then_inc(scattered[par][h], 16)

            for j in range(CH):
                n = slice(j * NT, (j + 1) * NT)
                p.wait_ge(hot_hi_ready, j + 1)
                tt(hot_val[:, n, 1, :], hot_hi[:, n], choice_b[:, n].unsqueeze(2).to_broadcast([P, NT, NCOL]),
                   ALU.mult).then_inc(hot_c_ready, 1)

            p.wait_ge(rows_ready, 1)
            p.wait_ge(bounds_ready, 1)
            last = p.value_load(bounds[0:1, E - 1:E], min_val=E, max_val=MAX_TILES)

            def take_waits(cell):
                tt(taken[:, cell:cell + 1], C("pcol", 1), C("pcol", 1), ALU.add)

            def gather(par, offsets):
                for h in range(HALVES):
                    nc.gpsimd.indirect_dma_start(
                        out=xg[:, par, h, :], out_offset=None, in_=xn_dram,
                        in_offset=bass.IndirectOffsetOnAxis(ap=offsets[:, h:h + 1], axis=0)).then_inc(gathered[par][h], 16)

            def take_lists(t, par, pair):
                p.wait_ge(x_moved, t + 2)
                for h in range(HALVES):
                    p.wait_ge(scattered[par][h], 16 * pair + 16 * (1 + par))
                nc.gpsimd.tensor_copy(lists_now[:, par], lists_all[:, bass.ds(t + AHEAD, 1)].rearrange(
                    "p o k h -> p (o k) h")).then_inc(lists_taken, 1)
                p.wait_ge(lists_taken, t + 1)

            def scatter(t, par):
                p.wait_ge(y_ready, t + 2)
                take_waits(1)
                for h in range(HALVES):
                    nc.gpsimd.indirect_dma_start(
                        out=y_dram, out_offset=bass.IndirectOffsetOnAxis(ap=lists_now[:, par, 1, h:h + 1], axis=0),
                        in_=y_sb[:, par, h, :], in_offset=None).then_inc(scattered[par][h], 16)

            p.wait_ge(xn_out, 64)
            gather(0, lists_all[:, 0, 0])
            gather(1, lists_all[:, 1, 0])
            p.wait_ge(x_moved, 1)
            gather(0, lists_all[:, 2, 0])
            p.wait_ge(rows_ready, 2)
            with p.Fori(0, last // 2) as i:
                for par in range(2):
                    t = 2 * i + par
                    take_lists(t, par, i)
                    take_waits(0)
                    gather(1 - par, lists_now[:, par, 0])
                    scatter(t, par)
            with p.If(last % 2 == 1):
                take_lists(last - 1, 0, last // 2)
                scatter(last - 1, 0)

        @block.tensor
        def _(pe):
            pe.sem_inc(act_ready, FC)
            pe.sem_inc(down_done, 1)
            pe.sem_inc(y_ready, 1)
            mm, tr = nc.tensor.matmul, nc.tensor.transpose
            ident = C("ident")
            pe.wait_ge(const_in, 16)
            pe.wait_ge(w_in, 48)
            for i in range(3):
                last = tr(bank[:, 6, i * D:(i + 1) * D], w_raw[:, i, :], ident)
            last.then_inc(w_turned, 1)
            pe.wait_ge(b1_in, 16)
            tr(bank[:, 5, 0:E * 2 * FC], b1_rows[:], ident[0:E * 2 * FC, 0:E * 2 * FC]).then_inc(b1_turned, 1)

            def nyquist(s, src, tiles):
                for t in tiles:
                    if s == 0:
                        pe.wait_ge(q_ready, t + 1)
                    last = mm(bank[:, 7, s * BATCH + 2 * t:s * BATCH + 2 * t + 2], src[:, t, :],
                              C("alt")[:, 2 * s:2 * s + 2], start=True, stop=True, skip_group_check=True)
                return last

            pe.wait_ge(ctx_in_s, 16)
            nyquist(1, ctx_sb, range(NT))

            def dft(g):
                if g >= 2:
                    pe.wait_ge(spec_ready, g - 1)
                y = bank[:, g % 2, :].rearrange("p (s r n) -> p s r n", s=2, r=2)
                for s, src in ((1, ctx_sb), (0, q_sb)):
                    if s == 0:
                        pe.wait_ge(q_ready, 2 * g + 2)
                    for j in range(2):
                        last = mm(y[:, s, :, 64 * j:64 * j + 64], src[:, 2 * g + j, :],
                                  C("fwd")[:, 128 * s:128 * s + 128].rearrange("p (r n) -> p r n", r=2), start=True, stop=True)
                last.then_inc(dft_done, 1)

            def project(g):
                pe.wait_ge(spec_ready, g + 1)
                if g >= 2:
                    pe.wait_ge(prod2_ready, g - 1)
                par = g % 2
                for i in range(3):
                    dst = bank[:, 2 + par, 256 * i:256 * i + 256] if i < 2 else bank[:, 4 + par, 0:256]
                    src = spec[:, par, min(i, 1)]
                    mm(dst, src[:, 0], basis[:, i, 0, :], start=True, stop=False)
                    mm(dst, src[:, 1], basis[:, i, 1, :], start=False, stop=False)
                    last = mm(dst, dc3[:], bbasis[:, i, :], start=False, stop=True)
                last.then_inc(proj_done, 1)

            def inverse(g):
                pe.wait_ge(sums_ready, g + 1)
                if g >= 2:
                    pe.wait_ge(x1_ready, g - 1)
                s = sums[:, g % 2, :].rearrange("p (n d) -> p n d", d=QUAD)
                inv = C("inv").rearrange("p (j m n) -> p j m n", j=2, m=3)
                for j in range(2):
                    at = bank[:, 6 + g % 2, 128 * j:128 * j + 128]
                    o = at.rearrange("p (q d) -> p q d", q=4)
                    mm(at, inv[:, j, 0], sums[:, g % 2, 4 * QUAD:8 * QUAD], start=True, stop=False, skip_group_check=True)
                    mm(o[:, 0:3:2], inv[:, j, 1], s[:, 3:12:8][:, ::-1], start=False, stop=False, skip_group_check=True)
                    mm(o[:, 1:4:2], inv[:, j, 2], s[:, 0:9:8][:, ::-1], start=False, stop=False, skip_group_check=True)
                    last = mm(at, nyq_inv[:, (2 * g + j) * P:(2 * g + j + 1) * P], sums_n[:, 4 * QUAD:8 * QUAD],
                              start=False, stop=True, skip_group_check=True)
                last.then_inc(att_done, 1)

            dft(0)
            nyquist(0, q_sb, range(0, 4))
            pe.wait_ge(basis_ready, 16)
            pe.wait_ge(bias_ready, 8)
            project(0)
            dft(1)
            nyquist(0, q_sb, range(4, 8))
            pe.wait_ge(b1_ready, 1)
            project(1)
            dft(2)
            nyquist(0, q_sb, range(8, NT)).then_inc(nyq_dft, 1)
            pe.wait_ge(nyq_spec, 1)
            for i in range(3):
                dst = bank[0:BATCH, 6, 256 * i:256 * i + 256] if i < 2 else bank[0:BATCH, 7, 128:384]
                last = mm(dst, spec_n[:, min(i, 1), :], basis[:, i, 0, :], start=True, stop=True)
            last.then_inc(nyq_proj, 1)
            pe.wait_ge(rest_in, 16)
            pe.wait_ge(nyq_in, 16)
            for g in range(1, G):
                if g + 1 < G:
                    project(g + 1)
                if g + 2 < G:
                    dft(g + 2)
                if g == 2:
                    pe.wait_ge(nyq_sums, 1)
                    inverse(0)
                if g >= 2:
                    inverse(g - 1)
            inverse(G - 1)

            pe.wait_ge(small_in, 48)
            pe.wait_ge(prod2_ready, G)
            def turn_xn(tiles):
                for t in tiles:
                    pe.wait_ge(xn_ready, t + 1)
                    last = tr(bank[:, t // 4, (t % 4) * P:(t % 4 + 1) * P], q_sb[:, t, :], ident)
                    if t % 4 == 3:
                        last.then_inc(xn_turned, 1)

            def gate(tiles):
                for t in tiles:
                    if t < NT // 2:
                        pe.wait_ge(xnT_first, t // 4 + 1)
                    else:
                        pe.wait_ge(xnT_ready, t // 4 - 1)
                    mm(bank[:, 4 + t // (NT // 2), t * E:(t + 1) * E], xnT[:, t, :], gw_sb[:], start=True, stop=True).then_inc(gate_done, 1)

            turn_xn(range(0, 8))
            gate(range(0, 3))
            turn_xn(range(8, 12))
            gate(range(3, 10))
            turn_xn(range(12, NT))
            gate(range(10, NT))
            pe.wait_ge(rowsum_ready, 1)
            mm(bank[:, 3, 0:E], tri_b[:], rowsum[:], start=True, stop=True)
            mm(bank[:, 3, E:2 * E], ones_b[:], rowsum[:], start=True, stop=True).then_inc(counted, 1)
            pe.wait_ge(bounds_ready, 1)
            ends = [pe.value_load(bounds[0:1, e:e + 1], min_val=e + 1, max_val=MAX_TILES) for e in range(E)]
            for n in range(CH * NT):
                if n in HOT_STARTS:
                    pe.wait_ge(hots_ready, HOT_STARTS.index(n) + 1)
                if n % NT == 0:
                    pe.wait_ge(hot_p_ready, n // NT + 1)
                    pe.wait_ge(hot_c_ready, n // NT + 1)
                last = mm(bank[:, 7, 0:2 * NCOL], hot_lo[:, n, :], hot_val[:, n].rearrange("p a c -> p (a c)"),
                          start=(n == 0), stop=(n == CH * NT - 1))
            last.then_inc(listed, 1)

            def turn_x():
                for h in range(HALVES):
                    last = tr(bank[:, 4, h * P:(h + 1) * P], x_now[:, h, :], ident)
                last.then_inc(xT_turned, 1)

            def keep_warm(times):
                for _ in range(times):
                    mm(bank[:, 0, 0:256], ident, C("fwd"), start=True, stop=True)

            keep_warm(8)
            pe.wait_ge(x_moved, 1)
            turn_x()
            keep_warm(2)
            pe.wait_ge(w1_ready, E)
            pe.wait_ge(w2_in, 16)
            for e in range(E):
                with pe.Fori(ends[e - 1] if e else 0, ends[e]) as t:
                    pe.wait_ge(xT_ready, t + 1)
                    for c in range(FC):
                        pe.wait_ge(act_ready, FC * t + c + 1)
                        for part in range(2):
                            dst = bank[:, c, part * XT:(part + 1) * XT]
                            cols = slice(part * FF + c * P, part * FF + (c + 1) * P)
                            mm(dst, w1_hi[:, e, cols], xT_hi[:], start=True, stop=False)
                            mm(dst, w1_hi[:, e, cols], xT_lo[:], start=False, stop=False)
                            last = mm(dst, w1_lo[:, e, cols], xT_hi[:], start=False, stop=True)
                        last.then_inc(up_done, 1)
                    pe.wait_ge(x_moved, t + 2)
                    turn_x()
                    pe.wait_ge(y_ready, t + 1)
                    for c in range(FC):
                        pe.wait_ge(act_ready, FC * t + FC + c + 1)
                        for h in range(HALVES):
                            last = mm(bank[:, 5 + h, 0:D], act[:, c, h * P:(h + 1) * P], w2_sb[:, e * FC + c, :],
                                      start=(c == 0), stop=(c == FC - 1))
                    last.then_inc(down_done, 1)


_INS = ["x", "ctx_1024", "L0_xattn_Wq", "L0_xattn_bq", "L0_xattn_Wk", "L0_xattn_bk", "L0_xattn_Wv", "L0_xattn_bv",
        "L0_ffn_gate_w", "L0_ffn_gate_b", "L0_ffn_w1", "L0_ffn_b1", "L0_ffn_w2", "L0_ffn_b2"]


def kernel(**inputs):
    import concourse.bacc as bacc
    from concourse.bass_utils import run_bass_kernel_spmd as run

    nc = bacc.Bacc("TRN2", target_bir_lowering=False, num_devices=1)
    arrays, args = {}, []
    for name in _INS:
        arr = np.ascontiguousarray(inputs[name])
        if name in ("x", "ctx_1024"):
            arr = arr.reshape(TOK, D)
        arrays[f"in_{name}"] = arr
        args.append(nc.dram_tensor(f"in_{name}", arr.shape, mybir.dt.from_np(arr.dtype), kind="ExternalInput").ap())
    cst, nyq, mem_scale = constants()
    for name, arr in (("const_table", cst), ("const_nyquist", nyq)):
        arrays[name] = arr
        args.append(nc.dram_tensor(name, arr.shape, F32, kind="ExternalInput").ap())
    out = nc.dram_tensor("out_0", (TOK, D), F32, kind="ExternalOutput").ap()
    build(nc, *args, out, mem_scale)
    r = run(nc, [arrays], core_ids=[0])
    return r.results[0]["out_0"].reshape(BATCH, SEQ, D)
```
